# Optimizing a Trainium2 kernel written in Bass

```python
import numpy as np
import jax
import jax.numpy as jnp

def _softmax(x, axis=-1):
    return jax.nn.softmax(x, axis=axis)

def _gelu(x):
    return jax.nn.gelu(x, approximate=True)

def _silu(x):
    return jax.nn.silu(x)

def _sigmoid(x):
    return jax.nn.sigmoid(x)

def _layernorm(x, axis=-1, eps=1e-05):
    m = jnp.mean(x, axis=axis, keepdims=True)
    v = jnp.var(x, axis=axis, keepdims=True)
    return (x - m) / jnp.sqrt(v + eps)

def _scatter_add(tgt, idx, src, axis=0):
    return tgt.at[idx].add(src)

def _segment_sum(src, seg, n):
    return jax.ops.segment_sum(src, seg, n)
kernel_name = 'mk_perceiver_d2_seqx_r4_9bcdda'

def setup_inputs(seed: int=0):
    np.random.seed(seed)
    _w = jnp.asarray

    def _rec_inputs():
        import jax
        import jax.numpy as jnp
        _rk = jax.random.key(seed)
        x = 7.22e-05 + 1 * jax.random.normal(jax.random.fold_in(_rk, 1), (32, 32, 512), jnp.float32)
        _lenS = 32 - jax.random.randint(jax.random.fold_in(_rk, 7), (32,), 0, max(1, 32 // 4) + 1, jnp.int32)
        _lenS2 = 257 - jax.random.randint(jax.random.fold_in(_rk, 8), (32,), 0, max(1, 257 // 4) + 1, jnp.int32)
        _ctx_512P = jax.random.normal(jax.random.fold_in(_rk, 11), (32, 16, 128), jnp.float32)
        _ctx_512c = jax.random.dirichlet(jax.random.fold_in(_rk, 511), 0.3 * jnp.ones((16,), jnp.float32), (32, 257))
        _ctx_512t = jnp.einsum('bsk,bkd->bsd', _ctx_512c, _ctx_512P)
        _ctx_512t = _ctx_512t * jax.lax.rsqrt(jnp.mean(jnp.square(_ctx_512t)) + 1e-12) * 0.953939
        ctx_512 = -0.000514642 + 1.00011 * (_ctx_512t + 0.3 * jax.random.normal(jax.random.fold_in(_rk, 611), (32, 257, 128), jnp.float32))
        return (x, ctx_512)
    x, ctx_512 = _rec_inputs()

    def _L0_xattn_setup():
        import jax, jax.numpy as jnp
        import numpy as np
        B, S, H, NH, L = (2, 512, 512, 16, 128)
        HD = H // NH
        key = jax.random.key(seed)
        k1, k2, k3, k4, k5 = jax.random.split(key, 5)
        scale = 0.02
        return {'q': jax.random.normal(k1, (B, S, H), dtype=jnp.float32), 'latent_kv': jax.random.normal(k2, (B, S, L), dtype=jnp.float32), 'Wq': jax.random.normal(k3, (H, H), dtype=jnp.float32) * scale, 'Wkv_expand': jax.random.normal(k4, (2 * H, L), dtype=jnp.float32) * scale, 'Wout': jax.random.normal(k5, (H, H), dtype=jnp.float32) * scale}
    _L0_xattn_all = _L0_xattn_setup()
    _L0_xattn_in = {k: v for k, v in _L0_xattn_all.items() if k in ('Wq', 'Wkv_expand', 'Wout')}
    del _L0_xattn_all

    def _L0_attn_setup():
        import jax, jax.numpy as jnp
        import numpy as np
        HID = 512
        H = 16
        D = HID // H
        THETA = 10000.0

        def _rope(q, k):
            T = q.shape[1]
            half = D // 2
            inv_freq = 1.0 / THETA ** (jnp.arange(half, dtype=jnp.float32) / half)
            ang = jnp.arange(T, dtype=jnp.float32)[:, None] * inv_freq[None, :]
            cos = jnp.cos(ang)[None, :, None, :]
            sin = jnp.sin(ang)[None, :, None, :]

            def rot(x):
                x1, x2 = (x[..., :half], x[..., half:])
                return jnp.concatenate([x1 * cos - x2 * sin, x2 * cos + x1 * sin], axis=-1)
            return (rot(q), rot(k))
        key = jax.random.key(seed)
        ks = jax.random.split(key, 7)
        B, T = (1, 512)
        s = 1.0 / np.sqrt(HID)
        return {'hidden_states': jax.random.normal(ks[0], (B, T, HID), dtype=jnp.float32), 'Wq': jax.random.normal(ks[1], (HID, HID), dtype=jnp.float32) * s, 'Wk': jax.random.normal(ks[2], (HID, HID), dtype=jnp.float32) * s, 'Wv': jax.random.normal(ks[3], (HID, HID), dtype=jnp.float32) * s, 'Wb': jax.random.normal(ks[4], (HID, H), dtype=jnp.float32) * s, 'bb': jnp.zeros((H,), dtype=jnp.float32), 'Wo': jax.random.normal(ks[5], (HID, HID), dtype=jnp.float32) * s}
    _L0_attn_all = _L0_attn_setup()
    _L0_attn_in = {k: v for k, v in _L0_attn_all.items() if k in ('Wq', 'Wk', 'Wv', 'Wb', 'bb', 'Wo')}
    del _L0_attn_all

    def _L0_ffn_setup():
        import jax, jax.numpy as jnp
        import numpy as np
        B, S, H, I = (1, 64, 512, 1536)

        def _quantized_matmul(x, w, scale):
            wq = w.astype(jnp.float8_e4m3fn).astype(x.dtype)
            y = jnp.einsum('bsi,io->bso', x, wq)
            return y * scale
        key = jax.random.key(seed)
        ks = jax.random.split(key, 7)
        return {'x': jax.random.normal(ks[0], (B, S, H), dtype=jnp.float32), 'gate_w': jax.random.normal(ks[1], (H, I), dtype=jnp.float32) * 0.02, 'up_w': jax.random.normal(ks[2], (H, I), dtype=jnp.float32) * 0.02, 'down_w': jax.random.normal(ks[3], (I, H), dtype=jnp.float32) * 0.02, 'gate_scale': jax.random.uniform(ks[4], (I,), dtype=jnp.float32, minval=0.5, maxval=1.5), 'up_scale': jax.random.uniform(ks[5], (I,), dtype=jnp.float32, minval=0.5, maxval=1.5), 'down_scale': jax.random.uniform(ks[6], (H,), dtype=jnp.float32, minval=0.5, maxval=1.5)}
    _L0_ffn_all = _L0_ffn_setup()
    _L0_ffn_in = {k: v for k, v in _L0_ffn_all.items() if k in ('gate_w', 'up_w', 'down_w', 'gate_scale', 'up_scale', 'down_scale')}
    del _L0_ffn_all

    def _L1_xattn_setup():
        import jax, jax.numpy as jnp
        import numpy as np
        B, S, H, NH, L = (2, 512, 512, 16, 128)
        HD = H // NH
        key = jax.random.key(seed)
        k1, k2, k3, k4, k5 = jax.random.split(key, 5)
        scale = 0.02
        return {'q': jax.random.normal(k1, (B, S, H), dtype=jnp.float32), 'latent_kv': jax.random.normal(k2, (B, S, L), dtype=jnp.float32), 'Wq': jax.random.normal(k3, (H, H), dtype=jnp.float32) * scale, 'Wkv_expand': jax.random.normal(k4, (2 * H, L), dtype=jnp.float32) * scale, 'Wout': jax.random.normal(k5, (H, H), dtype=jnp.float32) * scale}
    _L1_xattn_all = _L1_xattn_setup()
    _L1_xattn_in = {k: v for k, v in _L1_xattn_all.items() if k in ('Wq', 'Wkv_expand', 'Wout')}
    del _L1_xattn_all

    def _L1_attn_setup():
        import jax, jax.numpy as jnp
        import numpy as np
        B, S, D, H = (2, 512, 512, 16)
        HD = D // H
        NEG = jnp.float32(-1000000000.0)
        key = jax.random.key(seed)
        ks = jax.random.split(key, 6)
        slopes = np.array([2 ** (-8.0 * (i + 1) / H) for i in range(H)], dtype=np.float32)
        return {'hidden_states': jax.random.normal(ks[0], (B, S, D), jnp.float32), 'qkv_w': jax.random.normal(ks[1], (3 * D, D), jnp.float32) * (1.0 / np.sqrt(D)), 'qkv_b': jax.random.normal(ks[2], (3 * D,), jnp.float32) * 0.01, 'out_w': jax.random.normal(ks[3], (D, D), jnp.float32) * (1.0 / np.sqrt(D)), 'out_b': jax.random.normal(ks[4], (D,), jnp.float32) * 0.01, 'alibi_slopes': jnp.asarray(slopes)}
    _L1_attn_all = _L1_attn_setup()
    _L1_attn_in = {k: v for k, v in _L1_attn_all.items() if k in ('qkv_w', 'qkv_b', 'out_w', 'out_b', 'alibi_slopes')}
    del _L1_attn_all

    def _L1_ffn_setup():
        import jax, jax.numpy as jnp
        import numpy as np

        def binarize_weight(w):
            alpha = jnp.mean(jnp.abs(w), axis=tuple(range(1, w.ndim)), keepdims=True)
            bw = jnp.where(w >= 0, 1.0, -1.0) * alpha
            return jax.lax.stop_gradient(bw - w) + w
        key = jax.random.key(seed)
        k1, k2, k3 = jax.random.split(key, 3)
        in_features, out_features = (512, 512)
        x = jax.random.normal(k1, (8, 512, in_features), dtype=jnp.float32)
        std = np.sqrt(2.0 / out_features).astype(np.float32)
        weight = jax.random.normal(k2, (out_features, in_features), dtype=jnp.float32) * std
        bias = jax.random.normal(k3, (out_features,), dtype=jnp.float32) * 0.01
        return {'x': x, 'weight': weight, 'bias': bias}
    _L1_ffn_all = _L1_ffn_setup()
    _L1_ffn_in = {k: v for k, v in _L1_ffn_all.items() if k in ('weight', 'bias')}
    del _L1_ffn_all
    return {'x': x, 'ctx_512': ctx_512, 'L0_xattn_Wq': _L0_xattn_in['Wq'], 'L0_xattn_Wkv_expand': _L0_xattn_in['Wkv_expand'], 'L0_xattn_Wout': _L0_xattn_in['Wout'], 'L0_attn_Wq': _L0_attn_in['Wq'], 'L0_attn_Wk': _L0_attn_in['Wk'], 'L0_attn_Wv': _L0_attn_in['Wv'], 'L0_attn_Wb': _L0_attn_in['Wb'], 'L0_attn_bb': _L0_attn_in['bb'], 'L0_attn_Wo': _L0_attn_in['Wo'], 'L0_ffn_gate_w': _L0_ffn_in['gate_w'], 'L0_ffn_up_w': _L0_ffn_in['up_w'], 'L0_ffn_down_w': _L0_ffn_in['down_w'], 'L0_ffn_gate_scale': _L0_ffn_in['gate_scale'], 'L0_ffn_up_scale': _L0_ffn_in['up_scale'], 'L0_ffn_down_scale': _L0_ffn_in['down_scale'], 'L1_xattn_Wq': _L1_xattn_in['Wq'], 'L1_xattn_Wkv_expand': _L1_xattn_in['Wkv_expand'], 'L1_xattn_Wout': _L1_xattn_in['Wout'], 'L1_attn_qkv_w': _L1_attn_in['qkv_w'], 'L1_attn_qkv_b': _L1_attn_in['qkv_b'], 'L1_attn_out_w': _L1_attn_in['out_w'], 'L1_attn_out_b': _L1_attn_in['out_b'], 'L1_attn_alibi_slopes': _L1_attn_in['alibi_slopes'], 'L1_ffn_weight': _L1_ffn_in['weight'], 'L1_ffn_bias': _L1_ffn_in['bias']}

def reference(x, ctx_512, L0_xattn_Wq, L0_xattn_Wkv_expand, L0_xattn_Wout, L0_attn_Wq, L0_attn_Wk, L0_attn_Wv, L0_attn_Wb, L0_attn_bb, L0_attn_Wo, L0_ffn_gate_w, L0_ffn_up_w, L0_ffn_down_w, L0_ffn_gate_scale, L0_ffn_up_scale, L0_ffn_down_scale, L1_xattn_Wq, L1_xattn_Wkv_expand, L1_xattn_Wout, L1_attn_qkv_w, L1_attn_qkv_b, L1_attn_out_w, L1_attn_out_b, L1_attn_alibi_slopes, L1_ffn_weight, L1_ffn_bias):
    import jax
    import jax.numpy as jnp

    def _L0_xattn_ref(q, latent_kv, Wq, Wkv_expand, Wout):
        import jax, jax.numpy as jnp
        import numpy as np
        B, S, H, NH, L = (2, 512, 512, 16, 128)
        HD = H // NH
        b, sq, _ = q.shape
        sk = latent_kv.shape[1]
        qp = q @ Wq.T
        kv = latent_kv @ Wkv_expand.T
        k, v = jnp.split(kv, 2, axis=-1)
        qh = qp.reshape(b, sq, NH, HD).transpose(0, 2, 1, 3)
        kh = k.reshape(b, sk, NH, HD).transpose(0, 2, 1, 3)
        vh = v.reshape(b, sk, NH, HD).transpose(0, 2, 1, 3)
        inv_sqrt_d = 1.0 / jnp.sqrt(jnp.float32(HD))
        scores = jnp.einsum('bhqd,bhkd->bhqk', qh, kh) * inv_sqrt_d
        causal = jnp.tril(jnp.ones((sq, sk), dtype=bool))
        scores = jnp.where(causal, scores, jnp.finfo(scores.dtype).min)
        attn = jax.nn.softmax(scores, axis=-1)
        out = jnp.einsum('bhqk,bhkd->bhqd', attn, vh)
        out = out.transpose(0, 2, 1, 3).reshape(b, sq, H)
        return out @ Wout.T

    def _L0_attn_ref(hidden_states, Wq, Wk, Wv, Wb, bb, Wo):
        import jax, jax.numpy as jnp
        import numpy as np
        HID = 512
        H = 16
        D = HID // H
        THETA = 10000.0

        def _rope(q, k):
            T = q.shape[1]
            half = D // 2
            inv_freq = 1.0 / THETA ** (jnp.arange(half, dtype=jnp.float32) / half)
            ang = jnp.arange(T, dtype=jnp.float32)[:, None] * inv_freq[None, :]
            cos = jnp.cos(ang)[None, :, None, :]
            sin = jnp.sin(ang)[None, :, None, :]

            def rot(x):
                x1, x2 = (x[..., :half], x[..., half:])
                return jnp.concatenate([x1 * cos - x2 * sin, x2 * cos + x1 * sin], axis=-1)
            return (rot(q), rot(k))
        B, T, _ = hidden_states.shape
        scale = 1.0 / np.sqrt(D)
        q = (hidden_states @ Wq).reshape(B, T, H, D)
        k = (hidden_states @ Wk).reshape(B, T, H, D)
        v = (hidden_states @ Wv).reshape(B, T, H, D)
        beta = hidden_states @ Wb + bb
        q, k = _rope(q, k)
        s = jnp.einsum('bihd,bjhd->bhij', k, k) * scale
        idx = jnp.arange(T)
        strict = idx[:, None] > idx[None, :]
        s = jnp.where(strict, s, -jnp.inf)
        m = jnp.max(s, axis=-1, keepdims=True)
        e = jnp.exp(s - jnp.where(jnp.isfinite(m), m, 0.0))
        e = jnp.where(strict, e, 0.0)
        denom = jnp.sum(e, axis=-1, keepdims=True)
        p = e / jnp.where(denom == 0, 1.0, denom)
        L = p * beta.transpose(0, 2, 1)[..., None]
        A = L + jnp.eye(T, dtype=L.dtype)[None, None]
        u = jax.scipy.linalg.solve_triangular(A, v.transpose(0, 2, 1, 3), lower=True)
        sc = jnp.einsum('bihd,bjhd->bhij', q, k) * scale
        causal = idx[:, None] >= idx[None, :]
        sc = jnp.where(causal, sc, -jnp.inf)
        attn = jax.nn.softmax(sc, axis=-1)
        o = jnp.einsum('bhij,bhjd->bihd', attn, u).reshape(B, T, HID)
        return o @ Wo

    def _L0_ffn_ref(x, gate_w, up_w, down_w, gate_scale, up_scale, down_scale):
        import jax, jax.numpy as jnp
        import numpy as np
        B, S, H, I = (1, 64, 512, 1536)

        def _quantized_matmul(x, w, scale):
            wq = w.astype(jnp.float8_e4m3fn).astype(x.dtype)
            y = jnp.einsum('bsi,io->bso', x, wq)
            return y * scale
        gate = jax.nn.silu(_quantized_matmul(x, gate_w, gate_scale))
        up = _quantized_matmul(x, up_w, up_scale)
        fuse = gate * up
        return _quantized_matmul(fuse, down_w, down_scale)

    def _L1_xattn_ref(q, latent_kv, Wq, Wkv_expand, Wout):
        import jax, jax.numpy as jnp
        import numpy as np
        B, S, H, NH, L = (2, 512, 512, 16, 128)
        HD = H // NH
        b, sq, _ = q.shape
        sk = latent_kv.shape[1]
        qp = q @ Wq.T
        kv = latent_kv @ Wkv_expand.T
        k, v = jnp.split(kv, 2, axis=-1)
        qh = qp.reshape(b, sq, NH, HD).transpose(0, 2, 1, 3)
        kh = k.reshape(b, sk, NH, HD).transpose(0, 2, 1, 3)
        vh = v.reshape(b, sk, NH, HD).transpose(0, 2, 1, 3)
        inv_sqrt_d = 1.0 / jnp.sqrt(jnp.float32(HD))
        scores = jnp.einsum('bhqd,bhkd->bhqk', qh, kh) * inv_sqrt_d
        causal = jnp.tril(jnp.ones((sq, sk), dtype=bool))
        scores = jnp.where(causal, scores, jnp.finfo(scores.dtype).min)
        attn = jax.nn.softmax(scores, axis=-1)
        out = jnp.einsum('bhqk,bhkd->bhqd', attn, vh)
        out = out.transpose(0, 2, 1, 3).reshape(b, sq, H)
        return out @ Wout.T

    def _L1_attn_ref(hidden_states, qkv_w, qkv_b, out_w, out_b, alibi_slopes):
        import jax, jax.numpy as jnp
        import numpy as np
        B, S, D, H = (2, 512, 512, 16)
        HD = D // H
        NEG = jnp.float32(-1000000000.0)
        b, s, d = hidden_states.shape
        qkv = hidden_states @ qkv_w.T + qkv_b
        q, k, v = jnp.split(qkv, 3, axis=-1)
        q = q.reshape(b, s, H, HD)
        k = k.reshape(b, s, H, HD)
        v = v.reshape(b, s, H, HD)
        scale = 1.0 / np.sqrt(HD)
        scores = jnp.einsum('bqhd,bkhd->bhqk', q, k) * scale
        pos = jnp.arange(s)
        rel = (pos[None, :] - pos[:, None]).astype(jnp.float32)
        bias = alibi_slopes[:, None, None] * rel
        causal = pos[None, :] <= pos[:, None]
        scores = jnp.where(causal[None, None], scores + bias[None], NEG)
        attn = jax.nn.softmax(scores, axis=-1)
        out = jnp.einsum('bhqk,bkhd->bqhd', attn, v).reshape(b, s, d)
        out = out @ out_w.T + out_b
        return out

    def _L1_ffn_ref(x, weight, bias):
        import jax, jax.numpy as jnp
        import numpy as np

        def binarize_weight(w):
            alpha = jnp.mean(jnp.abs(w), axis=tuple(range(1, w.ndim)), keepdims=True)
            bw = jnp.where(w >= 0, 1.0, -1.0) * alpha
            return jax.lax.stop_gradient(bw - w) + w
        bw = binarize_weight(weight)
        return jnp.einsum('bsi,oi->bso', x, bw) + bias
    x = x + _L0_xattn_ref(_layernorm(x, axis=-1), ctx_512, L0_xattn_Wq, L0_xattn_Wkv_expand, L0_xattn_Wout)
    x = x + _L0_attn_ref(_layernorm(x, axis=-1), L0_attn_Wq, L0_attn_Wk, L0_attn_Wv, L0_attn_Wb, L0_attn_bb, L0_attn_Wo)
    x = x + _L0_ffn_ref(_layernorm(x, axis=-1), L0_ffn_gate_w, L0_ffn_up_w, L0_ffn_down_w, L0_ffn_gate_scale, L0_ffn_up_scale, L0_ffn_down_scale)
    x = x + _L1_xattn_ref(_layernorm(x, axis=-1), ctx_512, L1_xattn_Wq, L1_xattn_Wkv_expand, L1_xattn_Wout)
    x = x + _L1_attn_ref(_layernorm(x, axis=-1), L1_attn_qkv_w, L1_attn_qkv_b, L1_attn_out_w, L1_attn_out_b, L1_attn_alibi_slopes)
    x = x + _L1_ffn_ref(_layernorm(x, axis=-1), L1_ffn_weight, L1_ffn_bias)
    return x

_drawn_inputs = setup_inputs


def setup_inputs(seed=0):
    import zlib

    import numpy as np

    out = dict(_drawn_inputs(seed))
    spreads = {'L0_attn_bb': (0.0, 0.1)}
    factors = {'L0_xattn_Wq': 8.0,
     'L1_xattn_Wq': 23.389,
     'L1_attn_qkv_b': 6.922,
     'L1_attn_out_b': 7.539,
     'L1_ffn_bias': 8.0}
    for name, (base, spread) in spreads.items():
        noise = np.random.default_rng([zlib.crc32(name.encode()), seed]).standard_normal(out[name].shape)
        drawn = base * np.exp(spread * noise) if base else spread * noise
        out[name] = jnp.asarray(drawn.astype(out[name].dtype))
    for name, factor in factors.items():
        out[name] = (out[name] * factor).astype(out[name].dtype)
    return out
```

```python
from contextlib import ExitStack

import numpy as np
import concourse.bass as bass
from concourse import mybir

F32 = mybir.dt.float32
F32R = mybir.dt.float32r
FP8 = mybir.dt.float8e4
ALU = mybir.AluOpType
ACT = mybir.ActivationFunctionType
AX_X = mybir.AxisListType.X

P = 128
NB, S, H = 32, 32, 512
NH, HD = 16, 32
CTX_L, CTX_S = 128, 257
INNER = 1536
KT = H // P
TILES = NB * S // P
BPT = P // S
STAGES = ("x0", "a0", "f0", "x1", "a1", "f1")
ATTN = ("x0", "a0", "x1", "a1")
SOLVE_STEPS = 5
CHUNK = 2
MT = INNER // P
MASKED = -1e30
SCALE = float(1.0 / np.sqrt(np.float32(HD)))
EPS = 1e-5

C_IDENT, C_CAUSAL, C_STRICT, C_COS, C_SIN, C_REL, C_NOTFIRST, C_END = np.cumsum([0, P, S, S, HD, HD, S, 1])


def shape_constants():
    half = HD // 2
    c = np.zeros((P, C_END), np.float32)
    pos = np.arange(P) % S
    keys = np.arange(S)
    c[:, C_IDENT:C_CAUSAL] = np.eye(P)
    c[:, C_CAUSAL:C_STRICT] = np.where(keys[None] <= pos[:, None], 0.0, MASKED)
    c[:, C_STRICT:C_COS] = np.where(keys[None] < pos[:, None], 0.0, MASKED)
    inv_freq = np.float32(1.0) / np.float32(10000.0) ** (np.arange(half, dtype=np.float32) / np.float32(half))
    ang = pos.astype(np.float32)[:, None] * inv_freq[None]
    c[:, C_COS:C_SIN] = np.tile(np.cos(ang), (1, 2))
    c[:, C_SIN:C_REL] = np.concatenate([-np.sin(ang), np.sin(ang)], 1)
    c[:, C_REL:C_NOTFIRST] = (keys[None] - pos[:, None]).astype(np.float32)
    c[:, C_NOTFIRST] = pos > 0
    return c


SPLIT, QUANT, SIGN = "split", "quant", "sign"
UNITS = [("x0q", SPLIT, (0, 1)), ("x0kv", SPLIT, (2,)), ("x0o", SPLIT, (3, 4)),
         ("a0q", SPLIT, (5, 6)), ("a0k", SPLIT, (7, 8)), ("a0v", SPLIT, (9, 10)), ("a0o", SPLIT, (11, 12)),
         ("gate0", QUANT, (0,)), ("gate1", QUANT, (1,)), ("gate2", QUANT, (2,)),
         ("up0", QUANT, (3,)), ("up1", QUANT, (4,)), ("up2", QUANT, (13,)),
         ("down0", QUANT, (5,)), ("down1", QUANT, (6,)), ("down2", QUANT, (7,)),
         ("x1q", SPLIT, (8, 9)), ("x1kv", SPLIT, (10,)), ("x1o", SPLIT, (11, 12)),
         ("a1q", SPLIT, (0, 1)), ("a1k", SPLIT, (2, 3)), ("a1v", SPLIT, (4, 5)), ("a1o", SPLIT, (6, 7)),
         ("sign", SIGN, (13,))]
UNIT = {name: j for j, (name, _, _) in enumerate(UNITS)}
SLOTS = 14
FUSE_SLOTS = (10, 11, 12)
PREPARE_AT = {-4: ["x0q", "x0kv"], -1: ["x0o"], 1: ["a0q"], 2: ["a0k"], 3: ["a0v"], 4: ["a0o"],
              9: ["gate0"], 10: ["gate1"], 11: ["gate2"], 12: ["up0"], 13: ["up1"], 14: ["up2"],
              15: ["down0"], ("f0", 0, 4): ["down1"], ("f0", 0, 8): ["down2"],
              ("f0", 1): ["x1q"], ("f0", 3): ["x1kv", "x1o"],
              24: ["a1q"], 25: ["a1k"], 26: ["a1v"], 27: ["a1o"], 28: ["sign"]}
BETA_AT = 0
ALPHA_AT = 29


def kind(g):
    return STAGES[g // TILES]


def attn_index(g):
    return sum(kind(i) in ATTN for i in range(g))


def stage_tiles(name):
    s = STAGES.index(name)
    return range(s * TILES, (s + 1) * TILES)


def build(nc, x, ctxT, consts, w, vec, out):
    with ExitStack() as es:
        def sb(name, shape, dt=F32):
            return es.enter_context(nc.sbuf_tensor(name, shape, dt))

        def sem(name):
            return es.enter_context(nc.semaphore(name))

        wt = sb("wt", [P, SLOTS, KT * 512], F32R)
        raw = sb("raw", [P, 2, KT * 512])
        fp8 = sb("fp8", [P, 3, 1024], FP8)
        xres = sb("xres", [P, TILES, H])
        cst = sb("cst", [P, int(C_END)])
        ones = sb("ones", [P, P])
        neg_half = sb("neg_half", [P, 1])
        scale_bc = sb("scale_bc", [P, H])
        bias_bc = sb("bias_bc", [P, 2, H])
        gu_scale = sb("gu_scale", [P, 2, MT])
        small_bc = sb("small_bc", [P, 2, NH])
        beta_raw = sb("beta_raw", [P, KT, NH])
        beta_w = sb("beta_w", [P, 2, KT, NH], F32R)
        stats = sb("stats", [P, 2, 6])
        mean_var = sb("mean_var", [P, 2, 2])
        norm = sb("norm", [P, 2, 3])
        xn = sb("xn", [P, 2, H])
        a_hi = sb("a_hi", [P, 2, KT, P], F32R)
        a_lo = sb("a_lo", [P, 2, KT, P], F32R)
        ctx_raw = sb("ctx_raw", [P, 2, P])
        ctx_hi = sb("ctx_hi", [P, 2, P], F32R)
        ctx_lo = sb("ctx_lo", [P, 2, P], F32R)
        q_sb = sb("q_sb", [P, H])
        k_sb = sb("k_sb", [P, H])
        rot = sb("rot", [P, H])
        qT = sb("qT", [P, H])
        kT = sb("kT", [P, H])
        v_sb = sb("v_sb", [P, 2, H])
        beta = sb("beta", [P, 2, NH])
        sc = sb("sc", [P, 2, H])
        ex = sb("ex", [P, 2, H])
        row_max = sb("row_max", [P, 2, NH])
        den = sb("den", [P, 2, NH])
        rden = sb("rden", [P, 2, NH])
        lrow = sb("lrow", [P, NH])
        pT = sb("pT", [P, H])
        o_sb = sb("o_sb", [P, H])
        o_hi = sb("o_hi", [P, KT, P], F32R)
        o_lo = sb("o_lo", [P, KT, P], F32R)
        solve = sb("solve", [P, 3 * H])
        LU = solve[:, 0:2 * H].rearrange("p (h c) -> p h c", h=NH)
        LT = solve[:, 2 * H:3 * H]
        fuse = wt[:, FUSE_SLOTS[0]:FUSE_SLOTS[-1] + 1, :].rearrange(
            "p s n -> p (s n)").rearrange("p (a m t) -> p a m t", a=2, m=MT)

        ps = es.enter_context(nc.psum_tensor("ps", [P, 8, 512], F32))
        B_T, B_Q, B_K, B_V, B_S, B_KK, B_O, B_Y = range(8)
        B_KKS, B_QKS = B_S, B_S + 1
        GU_BANKS = (B_Q, B_K, B_V, B_O)

        x_loaded = [sem(f"x_loaded{i}") for i in range(2)]
        consts_loaded, bcast0_loaded = sem("consts_loaded"), sem("bcast0_loaded")
        f0_vec_loaded, a1_vec_loaded = sem("f0_vec_loaded"), sem("a1_vec_loaded")
        beta_raw_loaded = sem("beta_raw_loaded")
        raw_loaded = [sem(f"raw_loaded{i}") for i in range(2)]
        ctx_loaded = [sem(f"ctx_loaded{i}") for i in range(2)]
        pool_consts, pool_step = sem("pool_consts"), sem("pool_step")
        vec_step = sem("vec_step")
        w_hi, w_ready = sem("w_hi"), sem("w_ready")
        fp8_quarter, fp8_used = sem("fp8_quarter"), sem("fp8_used")
        sign_done, abs_done, alpha_mm, alpha_ready = sem("sign_done"), sem("abs_done"), sem("alpha_mm"), sem("alpha_ready")
        beta_hi, beta_w_ready = sem("beta_hi"), sem("beta_w_ready")
        stats_ready, rstd_ready, xn_ready = sem("stats_ready"), sem("rstd_ready"), sem("xn_ready")
        ln_T, a_hi_ready, a_ready = sem("ln_T"), sem("a_hi_ready"), sem("a_ready")
        ctx_hi_ready, ctx_ready = sem("ctx_hi_ready"), sem("ctx_ready")
        q_mm, k_mm, v_mm, beta_mm = sem("q_mm"), sem("k_mm"), sem("v_mm"), sem("beta_mm")
        qk_ready, v_ready, beta_ready = sem("qk_ready"), sem("v_ready"), sem("beta_ready")
        kk_mm, score_mm = sem("kk_mm"), sem("score_mm")
        kk_shifted, shifted, kk_exp, exp_done = sem("kk_shifted"), sem("shifted"), sem("kk_exp"), sem("exp_done")
        u0_ready, lt_ready, solve_mm, lt_next, l_next, u_done = (
            sem("u0_ready"), sem("lt_ready"), sem("solve_mm"), sem("lt_next"), sem("l_next"), sem("u_done"))
        p_ready, pv_mm, o_ready = sem("p_ready"), sem("pv_mm"), sem("o_ready")
        o_T, o_hi_ready, o_lo_ready, y_mm = sem("o_T"), sem("o_hi_ready"), sem("o_lo_ready"), sem("y_mm")
        x_new = sem("x_new")
        gu_mm, silu_ready, fused, fuse_hi, fuse_ready, down_mm = (
            sem("gu_mm"), sem("silu_ready"), sem("fused"), sem("fuse_hi"), sem("fuse_ready"), sem("down_mm"))
        sign_mm, stored = sem("sign_mm"), sem("stored")

        def heads(ap):
            return ap.rearrange("p (h c) -> p h c", h=NH)

        def per_head(ap):
            return ap.unsqueeze(2).broadcast_to([P, NH, S])

        def every_head(ap):
            return ap.unsqueeze(1).broadcast_to([P, NH, S])

        ident = cst[:, C_IDENT:C_CAUSAL]
        block = es.enter_context(nc.Block())

        A0 = stage_tiles("a0")
        RUN1, RUN2 = range(-3, 2 * TILES + 1), range(3 * TILES - 1, 6 * TILES + 1)

        def in_run(g, first=0):
            return 0 <= g < 6 * TILES and kind(g) != "f0"

        def is_attn(g):
            return in_run(g) and kind(g) in ATTN

        def a0_index(g):
            return g - A0[0]

        def attends_late(g):
            return is_attn(g) and kind(g) == "a0"

        def o_bank(g):
            return B_T if is_attn(g + 1) and kind(g + 1) == "a0" else B_KK

        def a0_before(g):
            return sum(1 for i in A0 if i < g)

        def ctx_index(g):
            return g if kind(g) == "x0" else TILES + g - stage_tiles("x1")[0]

        def ctx_tile(n):
            return n if n < TILES else stage_tiles("x1")[0] + n - TILES

        def normalised_here(g):
            return 0 <= g + 3 <= 2 * TILES + 2 or 3 * TILES + 2 <= g + 3 < 6 * TILES

        def transposed_here(g):
            return 0 <= g + 2 < 2 * TILES + CHUNK or 3 * TILES + CHUNK <= g + 2 < 6 * TILES

        def f0_normalised(c):
            return [g for g in range(2 * TILES + CHUNK * (c + 1), 2 * TILES + CHUNK * (c + 2)) if g > 2 * TILES + 2]

        def a_free(eng, g):
            if g < 2:
                return
            k = kind(g - 2)
            if k in ATTN:
                eng.wait_ge(v_mm, attn_index(g - 2) + 1)
                if k == "a0":
                    eng.wait_ge(beta_mm, a0_index(g - 2) + 1)
            elif k == "f0":
                eng.wait_ge(gu_mm, MT * ((g - 2 - 2 * TILES) // CHUNK + 1))
            else:
                eng.wait_ge(sign_mm, g - 2 - stage_tiles("f1")[0] + 1)

        def slots_free(eng, name):
            stage = name[:2]
            if name[:4] == "gate" or name in ("up0", "up1"):
                eng.wait_ge(v_mm, TILES)
                eng.wait_ge(y_mm, TILES)
            elif name[:4] == "down" or name == "x1q":
                eng.wait_ge(v_mm, 2 * TILES)
            elif name in ("x1kv", "x1o"):
                eng.wait_ge(down_mm, TILES)
            elif stage == "a1" or name == "sign":
                eng.wait_ge(gu_mm, MT * TILES // CHUNK)
                eng.wait_ge(down_mm, TILES)

        solve_out = ps[:, B_KKS:B_KKS + 2, :].rearrange("p b n -> p (b n)").rearrange("p (h c) -> p h c", h=NH)

        @block.sync
        def _(sp):
            xv = x.rearrange("(t p) d -> p t d", p=P)
            sp.dma_start(xres[:, 0:1, :], xv[:, 0:1, :]).then_inc(x_loaded[0], 16)
            sp.dma_start(cst[:], consts).then_inc(consts_loaded, 16)

            def load_unit(j):
                name, how, slots = UNITS[j]
                if j >= 2:
                    sp.wait_ge(w_ready, j - 1)
                dst = raw[:, j % 2, :]
                if name.endswith("kv"):
                    dst = dst[:, 0:1024]
                else:
                    dst = dst.rearrange("p (k n) -> p k n", k=KT)
                sp.dma_start(dst, w[name]).then_inc(raw_loaded[j % 2], 16)

            load_unit(0)
            load_unit(1)
            sp.dma_start(xres[:, 1:TILES, :], xv[:, 1:TILES, :]).then_inc(x_loaded[1], 16)
            sp.dma_start(beta_raw[:], vec["Wb"].rearrange("(k p) n -> p k n", p=P)).then_inc(beta_raw_loaded, 16)
            sp.dma_start(small_bc[:, 0, :], vec["bb"].partition_broadcast(P)).then_inc(bcast0_loaded, 16)
            sp.dma_start(small_bc[:, 1, :], vec["slopes"].partition_broadcast(P)).then_inc(bcast0_loaded, 16)
            sp.dma_start(scale_bc[:], vec["down_scale"].partition_broadcast(P)).then_inc(f0_vec_loaded, 16)
            sp.dma_start(gu_scale[:, 0, :], vec["gate_scale"]).then_inc(f0_vec_loaded, 16)
            sp.dma_start(gu_scale[:, 1, :], vec["up_scale"]).then_inc(f0_vec_loaded, 16)
            sp.dma_start(bias_bc[:, 0, :], vec["out_b"].partition_broadcast(P)).then_inc(bcast0_loaded, 16)
            sp.dma_start(bias_bc[:, 1, :], vec["ffn_b"].partition_broadcast(P)).then_inc(bcast0_loaded, 16)
            for j in range(2, UNIT["a1q"]):
                load_unit(j)
            sp.wait_ge(pv_mm, 2 * TILES)
            sp.dma_start(solve[:], vec["qkv_b"].partition_broadcast(P)).then_inc(a1_vec_loaded, 16)
            for j in range(UNIT["a1q"], len(UNITS)):
                load_unit(j)
            ov = out.rearrange("(t p) d -> p t d", p=P)
            for g in stage_tiles("f1"):
                sp.wait_ge(x_new, g + 1)
                sp.dma_start(ov[:, g % TILES, :], xres[:, g % TILES, :]).then_inc(stored, 16)
            sp.wait_ge(stored, 16 * TILES)

        @block.gpsimd
        def _(pool):
            steps = 0
            nc.gpsimd.memset(neg_half[:], -0.5).then_inc(pool_consts, 1)
            nc.gpsimd.memset(ones[:], 1.0).then_inc(pool_consts, 1)
            ctx_view = ctxT.rearrange("l (b k) -> l b k", k=CTX_S)

            def load_ctx(n):
                t = n % TILES
                if n >= 2:
                    pool.wait_ge(ctx_ready, n - 1)
                pool.dma_start(ctx_raw[:, n % 2, :].rearrange("p (b k) -> p b k", b=BPT),
                               ctx_view[:, BPT * t:BPT * (t + 1), 0:S]).then_inc(ctx_loaded[n % 2], 16)

            load_ctx(0)
            load_ctx(1)
            pool.wait_ge(pool_consts, 2)
            for g in range(6 * TILES):
                b = g % 2
                pool.wait_ge(stats_ready, g + 1)
                if g >= 2:
                    pool.wait_ge(xn_ready, g - 1)
                nc.gpsimd.tensor_scalar(norm[:, b, 0:1], mean_var[:, b, 1:2], EPS, None, ALU.add).then_inc(pool_step, 1)
                steps += 1
                pool.wait_ge(pool_step, steps)
                nc.gpsimd.tensor_tensor(norm[:, b, 1:2], norm[:, b, 0:1], neg_half[:], ALU.pow).then_inc(pool_step, 1)
                steps += 1
                pool.wait_ge(pool_step, steps)
                nc.gpsimd.tensor_scalar(norm[:, b, 2:3], mean_var[:, b, 0:1], -1.0, norm[:, b, 1:2],
                                        ALU.mult, ALU.mult).then_inc(rstd_ready, 1)
                for n in range(2, 2 * TILES):
                    if g == (n + 2 if n in (TILES, TILES + 1) else ctx_tile(n)):
                        load_ctx(n)

        @block.scalar
        def _(act):
            split_jobs = [0]
            quarters = [0]
            ctx_tiles = [0]

            def prepare(name):
                j = UNIT[name]
                _, how, slots = UNITS[j]
                act.wait_ge(raw_loaded[j % 2], 16 * (j // 2 + 1))
                slots_free(act, name)
                r = raw[:, j % 2, :]
                if how == SPLIT:
                    if name.endswith("kv"):
                        dst, r = wt[:, slots[0], 0:1024], r[:, 0:1024]
                    else:
                        dst = wt[:, slots[0], :]
                    nc.scalar.activation(dst, r, ACT.Copy).then_inc(w_hi, 1)
                elif how == QUANT:
                    for i in range(2):
                        if quarters[0]:
                            act.wait_ge(fp8_used, quarters[0])
                        nc.scalar.activation(fp8[:, 1, :], r[:, 1024 * i:1024 * (i + 1)], ACT.Copy,
                                             scale=0.25, saturate=False).then_inc(fp8_quarter, 1)
                        quarters[0] += 1
                else:
                    act.wait_ge(sign_done, 1)
                    nc.scalar.activation(r, r, ACT.Abs).then_inc(abs_done, 1)

            def normalise(g):
                act.wait_ge(rstd_ready, g + 1)
                if g >= 2:
                    act.wait_ge(ln_T, g - 1)
                nc.scalar.activation(xn[:, g % 2, :], xres[:, g % TILES, :], ACT.Identity,
                                     scale=norm[:, g % 2, 1:2], bias=norm[:, g % 2, 2:3]).then_inc(xn_ready, 1)

            def split_a(g):
                act.wait_ge(ln_T, g + 1)
                a_free(act, g)
                nc.scalar.activation(a_hi[:, g % 2, :, :], ps[:, B_T, :].rearrange("p (k t) -> p k t", k=KT),
                                     ACT.Copy).then_inc(a_hi_ready, 1)

            def split_ctx(g):
                n = ctx_tiles[0]
                ctx_tiles[0] += 1
                act.wait_ge(ctx_loaded[n % 2], 16 * (n // 2 + 1))
                if n >= 2:
                    act.wait_ge(v_mm, attn_index(ctx_tile(n - 2)) + 1)
                nc.scalar.activation(ctx_hi[:, n % 2, :], ctx_raw[:, n % 2, :], ACT.Copy).then_inc(ctx_hi_ready, 1)

            def slot(g):
                if is_attn(g):
                    a = attn_index(g)
                    if kind(g) == "a0":
                        act.wait_ge(kk_shifted, a0_index(g) + 1)
                        nc.scalar.activation(ex[:, 1, :], sc[:, 1, :], ACT.Exp).then_inc(kk_exp, 1)
                    act.wait_ge(shifted, a + 1)
                    nc.scalar.activation(ex[:, 0, :], sc[:, 0, :], ACT.Exp).then_inc(exp_done, 1)
                    if kind(g) == "a0":
                        act.wait_ge(v_ready, a + 1)
                        act.wait_ge(pv_mm, a)
                        nc.scalar.activation(LU[:, :, S:2 * S], heads(v_sb[:, g % 2, :]), ACT.Copy).then_inc(u0_ready, 1)
                if is_attn(g - 1):
                    a = attn_index(g - 1)
                    act.wait_ge(o_T, a + 1)
                    if a:
                        act.wait_ge(y_mm, a)
                    nc.scalar.activation(o_hi[:], ps[:, o_bank(g - 1), :].rearrange("p (k t) -> p k t", k=KT),
                                         ACT.Copy).then_inc(o_hi_ready, 1)
                if normalised_here(g):
                    normalise(g + 3)

                def l_copy(s):
                    n = a0_index(g) * (SOLVE_STEPS - 1) + s
                    act.wait_ge(lt_next, n + 1)
                    nc.scalar.activation(LU[:, :, 0:S], solve_out[:, :, 0:S], ACT.Copy).then_inc(l_next, 1)

                def take_v():
                    if is_attn(g + 1):
                        a = attn_index(g + 1)
                        if kind(g + 1) == "a1":
                            return
                        act.wait_ge(v_mm, a + 1)
                        if a >= 2:
                            act.wait_ge(pv_mm, a - 1)
                        if a >= TILES + 2:
                            act.wait_ge(u0_ready, min(a - 1 - TILES, TILES))
                        nc.scalar.activation(v_sb[:, (g + 1) % 2, :], ps[:, B_V, :], ACT.Copy).then_inc(v_ready, 1)

                def take_a():
                    if transposed_here(g):
                        if kind(g + 2)[0] == "x":
                            split_ctx(g + 2)
                        split_a(g + 2)

                if is_attn(g) and kind(g) == "a0":
                    l_copy(0)
                    l_copy(1)
                    l_copy(2)
                    take_v()
                    l_copy(3)
                    take_a()
                else:
                    take_v()
                    take_a()

            for name in PREPARE_AT[-4]:
                prepare(name)
            for g in RUN1:
                slot(g)
                if g == BETA_AT:
                    act.wait_ge(beta_raw_loaded, 16)
                    nc.scalar.activation(beta_w[:, 0], beta_raw[:], ACT.Copy).then_inc(beta_hi, 1)
                for name in PREPARE_AT.get(g, ()):
                    prepare(name)
            act.wait_ge(f0_vec_loaded, 48)
            for c in range(TILES // CHUNK):
                for g in f0_normalised(c):
                    normalise(g)
                for m in range(MT + 1):
                    n = c * MT + m
                    if m < MT:
                        act.wait_ge(gu_mm, n + 1)
                        if n >= 2:
                            act.wait_ge(fused, n - 1)
                        nc.scalar.activation(ex[:, m % 2, 0:CHUNK * P], ps[:, GU_BANKS[n % 4], 0:CHUNK * P], ACT.Silu,
                                             scale=gu_scale[:, 0, m:m + 1]).then_inc(silu_ready, 1)
                    if m:
                        act.wait_ge(fused, n)
                        if m == 1:
                            act.wait_ge(y_mm, 2 * TILES)
                            if c:
                                act.wait_ge(down_mm, CHUNK * c)
                        nc.scalar.activation(fuse[:, 0, m - 1, :], sc[:, (m - 1) % 2, 0:CHUNK * P],
                                             ACT.Copy).then_inc(fuse_hi, 1)
                    for name in PREPARE_AT.get(("f0", c, m), ()):
                        prepare(name)
                for i in range(CHUNK):
                    g = 2 * TILES + CHUNK * (c + 1) + i
                    if kind(g)[0] == "x":
                        split_ctx(g)
                    split_a(g)
                for name in PREPARE_AT.get(("f0", c), ()):
                    prepare(name)
            for g in RUN2:
                slot(g)
                for name in PREPARE_AT.get(g, ()):
                    prepare(name)

        @block.vector
        def _(dve):
            steps = [0]
            splits = [0]
            quarters = [0]
            ctx_tiles = [0]

            def step(ins):
                ins.then_inc(vec_step, 1)
                steps[0] += 1
                dve.wait_ge(vec_step, steps[0])

            def prepare(name):
                j = UNIT[name]
                _, how, slots = UNITS[j]
                r = raw[:, j % 2, :]
                if how == SPLIT:
                    splits[0] += 1
                    dve.wait_ge(w_hi, splits[0])
                    if name.endswith("kv"):
                        hi, lo, r = wt[:, slots[0], 0:1024], wt[:, slots[0], 1024:2048], r[:, 0:1024]
                    else:
                        hi, lo = wt[:, slots[0], :], wt[:, slots[1], :]
                    nc.vector.tensor_tensor(lo, r, hi.bitcast(F32), ALU.subtract).then_inc(w_ready, 1)
                elif how == QUANT:
                    dve.wait_ge(raw_loaded[j % 2], 16 * (j // 2 + 1))
                    slots_free(dve, name)
                    for i in range(2):
                        half = r[:, 1024 * i:1024 * (i + 1)]
                        step(nc.vector.tensor_scalar(fp8[:, 0, :], half, 240.0, -240.0, ALU.min, ALU.max, saturate=False))
                        quarters[0] += 1
                        dve.wait_ge(fp8_quarter, quarters[0])
                        step(nc.vector.tensor_scalar(fp8[:, 2, :], fp8[:, 1, :], 60.0, -60.0, ALU.min, ALU.max, saturate=False))
                        nc.vector.tensor_tensor(half, fp8[:, 1, :], fp8[:, 2, :], ALU.subtract).then_inc(fp8_used, 1)
                        dve.wait_ge(fp8_used, quarters[0])
                        last = nc.vector.scalar_tensor_tensor(
                            out=wt[:, slots[0], 1024 * i:1024 * (i + 1)], in0=half, scalar=4.0, in1=fp8[:, 0, :],
                            op0=ALU.mult, op1=ALU.add)
                        if i == 0:
                            step(last)
                    last.then_inc(w_ready, 1)
                    dve.wait_ge(w_ready, j + 1)
                else:
                    dve.wait_ge(raw_loaded[j % 2], 16 * (j // 2 + 1))
                    slots_free(dve, name)
                    dst = wt[:, slots[0], :]
                    step(nc.vector.tensor_scalar(dst, r, 0.0, 2.0, ALU.is_ge, ALU.mult))
                    nc.vector.tensor_scalar(dst, dst.bitcast(F32), -1.0, None, ALU.add).then_inc(sign_done, 1)

            def ln_stats(g):
                if g < TILES:
                    dve.wait_ge(x_loaded[min(g, 1)], 16)
                else:
                    dve.wait_ge(x_new, g - TILES + 1)
                if g >= 2:
                    dve.wait_ge(rstd_ready, g - 1)
                step(nc.vector.bn_stats(stats[:, g % 2, :], xres[:, g % TILES, :]))
                nc.vector.bn_aggr(mean_var[:, g % 2, :], stats[:, g % 2, :]).then_inc(stats_ready, 1)

            def split_a(g):
                dve.wait_ge(a_hi_ready, g + 1)
                nc.vector.tensor_tensor(a_lo[:, g % 2, :, :], ps[:, B_T, :].rearrange("p (k t) -> p k t", k=KT),
                                        a_hi[:, g % 2, :, :].bitcast(F32), ALU.subtract).then_inc(a_ready, 1)

            def split_ctx(g):
                n = ctx_tiles[0]
                ctx_tiles[0] += 1
                dve.wait_ge(ctx_hi_ready, n + 1)
                nc.vector.tensor_tensor(ctx_lo[:, n % 2, :], ctx_raw[:, n % 2, :], ctx_hi[:, n % 2, :].bitcast(F32),
                                        ALU.subtract).then_inc(ctx_ready, 1)

            def softmax_shift(bank, buf, mask, done):
                in1 = heads(rot[:]) if mask is None else every_head(mask)
                step(nc.vector.scalar_tensor_tensor(out=heads(sc[:, buf, :]), in0=heads(ps[:, bank, :]), scalar=SCALE,
                                                    in1=in1, op0=ALU.mult, op1=ALU.add))
                step(nc.vector.tensor_reduce(row_max[:, buf, :], heads(sc[:, buf, :]), AX_X, ALU.max))
                nc.vector.tensor_tensor(heads(sc[:, buf, :]), heads(sc[:, buf, :]), per_head(row_max[:, buf, :]),
                                        ALU.subtract).then_inc(done, 1)

            def rope(bank, dst):
                src = ps[:, bank, :].rearrange("p (h a c) -> p h a c", h=NH, a=2)
                halves = rot[:].rearrange("p (h a c) -> p h a c", h=NH, a=2)
                half = HD // 2
                nc.vector.tensor_tensor(heads(dst), heads(ps[:, bank, :]), every_head(cst[:, C_COS:C_SIN]), ALU.mult)
                for a in range(2):
                    sin = cst[:, C_SIN + half * a:C_SIN + half * (a + 1)]
                    last = nc.vector.tensor_tensor(halves[:, :, a, :], src[:, :, 1 - a, :],
                                                   sin.unsqueeze(1).broadcast_to([P, NH, half]), ALU.mult)
                step(last)
                step(nc.vector.tensor_tensor(dst, dst, rot[:], ALU.add))

            def take_q(g):
                if not is_attn(g):
                    return
                a = attn_index(g)
                dve.wait_ge(q_mm, a + 1)
                if a:
                    dve.wait_ge(score_mm, a)
                src = ps[:, B_Q, :]
                if kind(g) == "a0":
                    rope(B_Q, q_sb[:])
                    src = q_sb[:]
                elif kind(g) == "a1":
                    step(nc.vector.tensor_tensor(q_sb[:], src, solve[:, 0:H], ALU.add))
                    src = q_sb[:]
                step(nc.vector.transpose(qT[:], src))

            def take_k(g):
                if not is_attn(g):
                    return
                dve.wait_ge(k_mm, attn_index(g) + 1)
                src = ps[:, B_K, :]
                if kind(g) == "a0":
                    rope(B_K, k_sb[:])
                    src = k_sb[:]
                elif kind(g) == "a1":
                    step(nc.vector.tensor_tensor(k_sb[:], src, solve[:, H:2 * H], ALU.add))
                    src = k_sb[:]
                nc.vector.transpose(kT[:], src).then_inc(qk_ready, 1)

            def take_rest(g):
                if not in_run(g):
                    return
                if kind(g) == "a0":
                    n = a0_index(g)
                    dve.wait_ge(beta_mm, n + 1)
                    nc.vector.tensor_tensor(beta[:, g % 2, :], ps[:, B_O, 0:NH], small_bc[:, 0, :],
                                            ALU.add).then_inc(beta_ready, 1)
                elif kind(g) == "a1":
                    a = attn_index(g)
                    dve.wait_ge(v_mm, a + 1)
                    dve.wait_ge(pv_mm, a - 1)
                    nc.vector.tensor_tensor(v_sb[:, g % 2, :], ps[:, B_V, :], solve[:, 2 * H:3 * H],
                                            ALU.add).then_inc(v_ready, 1)

            def take_sign(g):
                if in_run(g) and kind(g) == "f1":
                    n = g - stage_tiles("f1")[0]
                    if n == 0:
                        dve.wait_ge(alpha_ready, 1)
                    dve.wait_ge(sign_mm, n + 1)
                    step(nc.vector.tensor_tensor(k_sb[:], ps[:, B_Q + g % 2, :], scale_bc[:], ALU.mult))
                    step(nc.vector.tensor_tensor(k_sb[:], k_sb[:], bias_bc[:, 1, :], ALU.add))
                    nc.vector.tensor_tensor(xres[:, g % TILES, :], xres[:, g % TILES, :], k_sb[:],
                                            ALU.add).then_inc(x_new, 1)
                    dve.wait_ge(x_new, g + 1)

            def residual(g):
                if not is_attn(g):
                    return
                t = g % TILES
                dve.wait_ge(y_mm, attn_index(g) + 1)
                if kind(g) == "a1":
                    step(nc.vector.tensor_tensor(xres[:, t, :], xres[:, t, :], bias_bc[:, 0, :], ALU.add))
                nc.vector.tensor_tensor(xres[:, t, :], xres[:, t, :], ps[:, B_Y, :], ALU.add).then_inc(x_new, 1)

            def take_a(g):
                if transposed_here(g - 2):
                    if kind(g)[0] == "x":
                        split_ctx(g)
                    split_a(g)

            def stats_next(g):
                if normalised_here(g):
                    ln_stats(g + 3)

            def o_norm(g):
                if is_attn(g):
                    a = attn_index(g)
                    dve.wait_ge(pv_mm, a + 1)
                    if a:
                        dve.wait_ge(o_T, a)
                    nc.vector.tensor_tensor(heads(o_sb[:]), heads(ps[:, B_O, :]), per_head(rden[:, 0, :]),
                                            ALU.mult).then_inc(o_ready, 1)

            def split_o(g):
                if is_attn(g):
                    dve.wait_ge(o_hi_ready, attn_index(g) + 1)
                    nc.vector.tensor_tensor(o_lo[:], ps[:, o_bank(g), :].rearrange("p (k t) -> p k t", k=KT),
                                            o_hi[:].bitcast(F32), ALU.subtract).then_inc(o_lo_ready, 1)

            def slot(g):
                if not attends_late(g - 1):
                    o_norm(g - 1)
                if is_attn(g):
                    a = attn_index(g)
                    if kind(g) == "a0":
                        dve.wait_ge(kk_mm, a0_index(g) + 1)
                        softmax_shift(B_KKS, 1, cst[:, C_STRICT:C_COS], kk_shifted)
                        bank = B_QKS
                    else:
                        bank = B_S
                    dve.wait_ge(score_mm, a + 1)
                    mask = None if kind(g) == "a1" else cst[:, C_CAUSAL:C_STRICT]
                    if g == stage_tiles("a1")[0]:
                        for h in range(NH):
                            last = nc.vector.scalar_tensor_tensor(
                                out=rot[:, S * h:S * (h + 1)], in0=cst[:, C_REL:C_NOTFIRST], scalar=small_bc[:, 1, h:h + 1],
                                in1=cst[:, C_CAUSAL:C_STRICT], op0=ALU.mult, op1=ALU.add)
                        step(last)
                    softmax_shift(bank, 0, mask, shifted)
                if attends_late(g - 1):
                    o_norm(g - 1)
                if is_attn(g) and kind(g) == "a0":
                    n = a0_index(g)
                    dve.wait_ge(kk_exp, n + 1)
                    step(nc.vector.tensor_reduce(den[:, 1, :], heads(ex[:, 1, :]), AX_X, ALU.add))
                    step(nc.vector.reciprocal(rden[:, 1, :], den[:, 1, :]))
                    dve.wait_ge(beta_ready, n + 1)
                    step(nc.vector.scalar_tensor_tensor(out=lrow[:], in0=rden[:, 1, :],
                                                        scalar=cst[:, C_NOTFIRST:C_END], in1=beta[:, g % 2, :],
                                                        op0=ALU.mult, op1=ALU.mult))
                    step(nc.vector.tensor_tensor(LU[:, :, 0:S], heads(ex[:, 1, :]), per_head(lrow[:]), ALU.mult))
                    nc.vector.transpose(heads(LT), LU[:, :, 0:S]).then_inc(lt_ready, 1)
                else:
                    split_o(g - 1)
                if is_attn(g):
                    a = attn_index(g)
                    dve.wait_ge(exp_done, a + 1)
                    if a:
                        dve.wait_ge(pv_mm, a)
                    nc.vector.transpose(pT[:], ex[:, 0, :]).then_inc(p_ready, 1)
                    step(nc.vector.tensor_reduce(den[:, 0, :], heads(ex[:, 0, :]), AX_X, ALU.add))
                    step(nc.vector.reciprocal(rden[:, 0, :], den[:, 0, :]))
                if is_attn(g) and kind(g) == "a0":
                    split_o(g - 1)

                def solve_step(s):
                    n = a0_index(g) * SOLVE_STEPS + s
                    dve.wait_ge(solve_mm, n + 1)
                    if s == 0:
                        dve.wait_ge(u0_ready, a0_index(g) + 1)
                    last = s == SOLVE_STEPS - 1
                    ins = nc.vector.tensor_tensor(
                        LU[:, :, S:2 * S], LU[:, :, S:2 * S], solve_out[:, :, S:2 * S],
                        ALU.subtract if s == 0 else ALU.add)
                    if last:
                        ins.then_inc(u_done, 1)
                    else:
                        nc.vector.transpose(heads(LT), solve_out[:, :, 0:S]).then_inc(lt_next, 1)

                stats_next(g)
                if is_attn(g) and kind(g) == "a0":
                    solve_step(0)
                    take_q(g + 1)
                    residual(g - 1)
                    solve_step(1)
                    solve_step(2)
                    take_k(g + 1)
                    solve_step(3)
                    take_rest(g + 1)
                    take_a(g + 2)
                    solve_step(4)
                else:
                    take_q(g + 1)
                    take_k(g + 1)
                    take_rest(g + 1)
                    take_a(g + 2)
                    residual(g - 1)
                    take_sign(g)

            for name in PREPARE_AT[-4]:
                prepare(name)
            dve.wait_ge(consts_loaded, 16)
            dve.wait_ge(bcast0_loaded, 64)
            for g in RUN1:
                slot(g)
                if g == BETA_AT:
                    dve.wait_ge(beta_hi, 1)
                    nc.vector.tensor_tensor(beta_w[:, 1], beta_raw[:], beta_w[:, 0].bitcast(F32),
                                            ALU.subtract).then_inc(beta_w_ready, 1)
                for name in PREPARE_AT.get(g, ()):
                    prepare(name)
            dve.wait_ge(f0_vec_loaded, 48)
            for c in range(TILES // CHUNK):
                for g in f0_normalised(c):
                    ln_stats(g)
                for m in range(MT + 1):
                    n = c * MT + m
                    if m < MT:
                        dve.wait_ge(silu_ready, n + 1)
                        if n >= 2:
                            dve.wait_ge(fuse_hi, n - 1)
                            dve.wait_ge(fuse_ready, n - 1)
                        nc.vector.scalar_tensor_tensor(
                            out=sc[:, m % 2, 0:CHUNK * P], in0=ps[:, GU_BANKS[n % 4], CHUNK * P:2 * CHUNK * P],
                            scalar=gu_scale[:, 1, m:m + 1], in1=ex[:, m % 2, 0:CHUNK * P], op0=ALU.mult,
                            op1=ALU.mult).then_inc(fused, 1)
                    if m:
                        dve.wait_ge(fuse_hi, n)
                        nc.vector.tensor_tensor(fuse[:, 1, m - 1, :], sc[:, (m - 1) % 2, 0:CHUNK * P],
                                                fuse[:, 0, m - 1, :].bitcast(F32), ALU.subtract).then_inc(fuse_ready, 1)
                    for name in PREPARE_AT.get(("f0", c, m), ()):
                        prepare(name)
                for i in range(CHUNK):
                    g = 2 * TILES + CHUNK * (c + 1) + i
                    if kind(g)[0] == "x":
                        split_ctx(g)
                    split_a(g)
                for i in range(CHUNK):
                    g = 2 * TILES + CHUNK * c + i
                    dve.wait_ge(down_mm, CHUNK * c + i + 1)
                    step(nc.vector.tensor_tensor(k_sb[:], ps[:, B_S + i, :], scale_bc[:], ALU.mult))
                    nc.vector.tensor_tensor(xres[:, g % TILES, :], xres[:, g % TILES, :], k_sb[:],
                                            ALU.add).then_inc(x_new, 1)
                    dve.wait_ge(x_new, g + 1)
                for name in PREPARE_AT.get(("f0", c), ()):
                    prepare(name)
            dve.wait_ge(a1_vec_loaded, 16)
            for g in RUN2:
                slot(g)
                for name in PREPARE_AT.get(g, ()):
                    prepare(name)
                if g == ALPHA_AT:
                    dve.wait_ge(alpha_mm, 1)
                    nc.vector.tensor_scalar(scale_bc[:], ps[:, B_Y, :], 1.0 / H, None, ALU.mult).then_inc(alpha_ready, 1)

        @block.tensor
        def _(pe):
            issued = {"ln_T": 0, "o_T": 0}

            def mm3(dst, hi, lo, w_hi_of, w_lo_of, nk):
                for k in range(nk):
                    nc.tensor.matmul(dst, hi(k), w_hi_of(k), start=(k == 0), stop=False)
                    nc.tensor.matmul(dst, hi(k), w_lo_of(k), start=False, stop=False)
                    last = nc.tensor.matmul(dst, lo(k), w_hi_of(k), start=False, stop=(k == nk - 1))
                return last

            def weight(slot, k):
                return wt[:, slot, 512 * k:512 * (k + 1)]

            def bank_T_free():
                if issued["ln_T"]:
                    pe.wait_ge(a_ready, issued["ln_T"])
                if issued["o_T"]:
                    pe.wait_ge(o_lo_ready, issued["o_T"])

            def ln_transpose(g):
                pe.wait_ge(xn_ready, g + 1)
                bank_T_free()
                for k in range(KT):
                    last = nc.tensor.transpose(ps[:, B_T, P * k:P * (k + 1)], xn[:, g % 2, P * k:P * (k + 1)], ident)
                last.then_inc(ln_T, 1)
                issued["ln_T"] += 1

            def project(name, g, bank, done):
                hi_slot, lo_slot = UNITS[UNIT[name]][2]
                pe.wait_ge(w_ready, UNIT[name] + 1)
                pe.wait_ge(a_ready, g + 1)
                mm3(ps[:, bank, :], lambda k: a_hi[:, g % 2, k, :], lambda k: a_lo[:, g % 2, k, :],
                    lambda k: weight(hi_slot, k), lambda k: weight(lo_slot, k), KT).then_inc(done, 1)

            def q_project(g):
                if not is_attn(g):
                    return
                a = attn_index(g)
                if a:
                    pe.wait_ge(qk_ready, a)
                if a == 2 * TILES:
                    pe.wait_ge(fused, MT * TILES // CHUNK)
                project(kind(g) + "q", g, B_Q, q_mm)

            def k_project(g):
                if not is_attn(g):
                    return
                if kind(g)[0] == "x":
                    n = ctx_index(g)
                    pe.wait_ge(ctx_ready, n + 1)
                    pe.wait_ge(w_ready, UNIT[kind(g) + "kv"] + 1)
                    slot, b = UNITS[UNIT[kind(g) + "kv"]][2][0], n % 2
                    mm3(ps[:, B_K, :], lambda k: ctx_hi[:, b, :], lambda k: ctx_lo[:, b, :],
                        lambda k: wt[:, slot, 0:512], lambda k: wt[:, slot, 1024:1536], 1).then_inc(k_mm, 1)
                else:
                    project(kind(g) + "k", g, B_K, k_mm)

            def v_project(g):
                if not is_attn(g):
                    return
                a = attn_index(g)
                if a:
                    pe.wait_ge(v_ready, a)
                if kind(g)[0] == "x":
                    b = ctx_index(g) % 2
                    slot = UNITS[UNIT[kind(g) + "kv"]][2][0]
                    mm3(ps[:, B_V, :], lambda k: ctx_hi[:, b, :], lambda k: ctx_lo[:, b, :],
                        lambda k: wt[:, slot, 512:1024], lambda k: wt[:, slot, 1536:2048], 1).then_inc(v_mm, 1)
                else:
                    project(kind(g) + "v", g, B_V, v_mm)

            def beta_project(g):
                if is_attn(g) and kind(g) == "a0":
                    a = attn_index(g)
                    pe.wait_ge(beta_w_ready, 1)
                    pe.wait_ge(o_ready, a - 1)
                    mm3(ps[:, B_O, 0:NH], lambda k: a_hi[:, g % 2, k, :], lambda k: a_lo[:, g % 2, k, :],
                        lambda k: beta_w[:, 0, k, :], lambda k: beta_w[:, 1, k, :], KT).then_inc(beta_mm, 1)

            def sign_project(g):
                if not (in_run(g) and kind(g) == "f1"):
                    return
                n = g - stage_tiles("f1")[0]
                pe.wait_ge(sign_done, 1)
                pe.wait_ge(a_ready, g + 1)
                if n == 0:
                    pe.wait_ge(qk_ready, 4 * TILES)
                if n >= 2:
                    pe.wait_ge(x_new, g - 1)
                for k in range(KT):
                    for j, part in enumerate((a_hi, a_lo)):
                        last = nc.tensor.matmul(ps[:, B_Q + g % 2, :], part[:, g % 2, k, :],
                                                weight(UNITS[UNIT["sign"]][2][0], k), start=(k == 0 and j == 0),
                                                stop=(k == KT - 1 and j == 1))
                last.then_inc(sign_mm, 1)

            def blocks(dst, lhs, rhs):
                for h in range(NH):
                    for b in range(BPT):
                        rows = slice(S * b, S * (b + 1))
                        last = nc.tensor.matmul(dst(h, rows), lhs(h, rows), rhs(h, rows), start=True, stop=True)
                return last

            def col(ap):
                return lambda h, rows: ap[rows, S * h:S * (h + 1)]

            def score(g):
                a = attn_index(g)
                pe.wait_ge(qk_ready, a + 1)
                if a0_before(g):
                    pe.wait_ge(u_done, a0_before(g))
                if a == 2 * TILES:
                    pe.wait_ge(x_new, 3 * TILES)
                if a:
                    pe.wait_ge(shifted, a)
                if kind(g) == "a0":
                    pe.wait_ge(o_lo_ready, a - 1)
                    blocks(col(ps[:, B_KKS, :]), col(kT), col(kT)).then_inc(kk_mm, 1)
                blocks(col(ps[:, B_QKS if kind(g) == "a0" else B_S, :]), col(qT), col(kT)).then_inc(score_mm, 1)

            def o_transpose(g):
                if not is_attn(g):
                    return
                pe.wait_ge(o_ready, attn_index(g) + 1)
                if o_bank(g) == B_T:
                    bank_T_free()
                else:
                    pe.wait_ge(o_lo_ready, attn_index(g))
                for k in range(KT):
                    last = nc.tensor.transpose(ps[:, o_bank(g), P * k:P * (k + 1)], o_sb[:, P * k:P * (k + 1)], ident)
                last.then_inc(o_T, 1)
                issued["o_T"] += 1

            def out_project(g):
                if not is_attn(g):
                    return
                hi_slot, lo_slot = UNITS[UNIT[kind(g) + "o"]][2]
                pe.wait_ge(w_ready, UNIT[kind(g) + "o"] + 1)
                pe.wait_ge(o_lo_ready, attn_index(g) + 1)
                if g:
                    pe.wait_ge(x_new, g)
                if g == ALPHA_AT:
                    pe.wait_ge(alpha_ready, 1)
                mm3(ps[:, B_Y, :], lambda k: o_hi[:, k, :], lambda k: o_lo[:, k, :],
                    lambda k: weight(hi_slot, k), lambda k: weight(lo_slot, k), KT).then_inc(y_mm, 1)

            def solve_step(g, s):
                n = a0_index(g)
                if s == 0:
                    pe.wait_ge(lt_ready, n + 1)
                    pe.wait_ge(u0_ready, n + 1)
                    pe.wait_ge(shifted, attn_index(g) + 1)
                else:
                    pe.wait_ge(l_next, n * (SOLVE_STEPS - 1) + s)
                if s < SOLVE_STEPS - 1:
                    last = blocks(lambda h, r: solve_out[r, h, :], col(LT), lambda h, r: LU[r, h, :])
                else:
                    last = blocks(lambda h, r: solve_out[r, h, S:2 * S], col(LT), lambda h, r: LU[r, h, S:2 * S])
                last.then_inc(solve_mm, 1)

            def attend(g):
                a = attn_index(g)
                pe.wait_ge(p_ready, a + 1)
                if a:
                    pe.wait_ge(o_ready, a)
                if a == 2 * TILES:
                    pe.wait_ge(fused, MT * TILES // CHUNK)
                if kind(g) == "a0":
                    pe.wait_ge(u_done, a0_index(g) + 1)
                    rhs = lambda h, r: LU[r, h, S:2 * S]
                else:
                    pe.wait_ge(v_ready, a + 1)
                    rhs = lambda h, r: v_sb[r, g % 2, S * h:S * (h + 1)]
                if g + 1 in A0:
                    pe.wait_ge(beta_ready, a0_index(g + 1) + 1)
                blocks(col(ps[:, B_O, :]), col(pT), rhs).then_inc(pv_mm, 1)

            def slot(g):
                if is_attn(g):
                    score(g)
                if attends_late(g - 1):
                    attend(g - 1)
                q_project(g + 1)
                o_transpose(g - 1)
                if is_attn(g) and kind(g) == "a0":
                    solve_step(g, 0)
                    out_project(g - 1)
                    solve_step(g, 1)
                    k_project(g + 1)
                    solve_step(g, 2)
                    v_project(g + 1)
                    solve_step(g, 3)
                    beta_project(g + 1)
                    if transposed_here(g):
                        ln_transpose(g + 2)
                    solve_step(g, 4)
                else:
                    k_project(g + 1)
                    v_project(g + 1)
                    beta_project(g + 1)
                    if transposed_here(g):
                        ln_transpose(g + 2)
                    out_project(g - 1)
                    sign_project(g)
                if is_attn(g) and not attends_late(g):
                    attend(g)

            pe.wait_ge(consts_loaded, 16)
            for g in RUN1:
                slot(g)
            for c in range(TILES // CHUNK):
                for m in range(MT):
                    n = c * MT + m
                    bank = GU_BANKS[n % 4]
                    if n == 0:
                        pe.wait_ge(v_ready, 2 * TILES)
                        pe.wait_ge(o_ready, 2 * TILES)
                    if n >= 4:
                        pe.wait_ge(fused, n - 3)
                    if m == 0:
                        pe.wait_ge(a_ready, 2 * TILES + CHUNK * (c + 1))
                    for half, which in enumerate(("gate", "up")):
                        unit = UNIT[which + str(m // 4)]
                        pe.wait_ge(w_ready, unit + 1)
                        for k in range(KT):
                            for j, part in enumerate((a_hi, a_lo)):
                                col0 = 512 * k + P * (m % 4)
                                last = nc.tensor.matmul(
                                    ps[:, bank, CHUNK * P * half:CHUNK * P * (half + 1)],
                                    wt[:, UNITS[unit][2][0], col0:col0 + P], part[:, :, k, :],
                                    start=(k == 0 and j == 0), stop=(k == KT - 1 and j == 1))
                    last.then_inc(gu_mm, 1)
                for i in range(CHUNK):
                    ln_transpose(2 * TILES + CHUNK * (c + 1) + i)
                for i in range(CHUNK):
                    n = CHUNK * c + i
                    if c == 0:
                        pe.wait_ge(u_done, TILES)
                    else:
                        pe.wait_ge(x_new, 2 * TILES + n - 1)
                    if i == 0:
                        pe.wait_ge(fuse_ready, MT * (c + 1))
                    for m in range(MT):
                        unit = UNIT["down" + str(m // 4)]
                        pe.wait_ge(w_ready, unit + 1)
                        for j in range(2):
                            last = nc.tensor.matmul(ps[:, B_S + i, :], fuse[:, j, m, P * i:P * (i + 1)],
                                                    weight(UNITS[unit][2][0], m % 4), start=(m == 0 and j == 0),
                                                    stop=(m == MT - 1 and j == 1))
                    last.then_inc(down_mm, 1)
            for g in RUN2:
                slot(g)
                if g == ALPHA_AT:
                    pe.wait_ge(abs_done, 1)
                    pe.wait_ge(pool_consts, 2)
                    pe.wait_ge(x_new, g)
                    for k in range(KT):
                        last = nc.tensor.matmul(ps[:, B_Y, :], ones[:], raw[:, UNIT["sign"] % 2, 512 * k:512 * (k + 1)],
                                                start=(k == 0), stop=(k == KT - 1))
                    last.then_inc(alpha_mm, 1)


def kernel(**inputs):
    import concourse.bacc as bacc
    from concourse.bass_utils import run_bass_kernel_spmd

    a = {k: np.asarray(v) for k, v in inputs.items()}
    nc = bacc.Bacc("TRN2", target_bir_lowering=False, num_devices=1)
    feed = {}

    def dram(name, array):
        feed[name] = np.ascontiguousarray(array)
        return nc.dram_tensor(name, feed[name].shape, mybir.dt.from_np(feed[name].dtype), kind="ExternalInput").ap()

    def units(ap, names, rows):
        blocks = {}
        for i, name in enumerate(names):
            part = ap[512 * i:512 * (i + 1), :] if rows else ap[:, 512 * i:512 * (i + 1)]
            blocks[name] = part.rearrange("(k p) n -> p k n", p=P)
        return blocks

    w = {}
    for s in "01":
        w |= units(dram(f"x{s}_wq", a[f"L{s}_xattn_Wq"].T), [f"x{s}q"], False)
        w[f"x{s}kv"] = dram(f"x{s}_wkv", a[f"L{s}_xattn_Wkv_expand"].T)
        w |= units(dram(f"x{s}_wo", a[f"L{s}_xattn_Wout"].T), [f"x{s}o"], False)
    for c in "qkvo":
        w |= units(dram(f"a0_w{c}", a[f"L0_attn_W{c}"]), [f"a0{c}"], False)
    w |= units(dram("gate_w", a["L0_ffn_gate_w"]), ["gate0", "gate1", "gate2"], False)
    w |= units(dram("up_w", a["L0_ffn_up_w"]), ["up0", "up1", "up2"], False)
    w |= units(dram("down_w", a["L0_ffn_down_w"]), ["down0", "down1", "down2"], True)
    w |= units(dram("a1_wqkv", a["L1_attn_qkv_w"].T), ["a1q", "a1k", "a1v"], False)
    w |= units(dram("a1_wo", a["L1_attn_out_w"].T), ["a1o"], False)
    w |= units(dram("f1_w", a["L1_ffn_weight"].T), ["sign"], False)
    vec = {
        "Wb": dram("Wb", a["L0_attn_Wb"]), "bb": dram("bb", a["L0_attn_bb"]),
        "slopes": dram("slopes", a["L1_attn_alibi_slopes"]), "down_scale": dram("down_scale", a["L0_ffn_down_scale"]),
        "gate_scale": dram("gate_scale", a["L0_ffn_gate_scale"].reshape(MT, P).T),
        "up_scale": dram("up_scale", a["L0_ffn_up_scale"].reshape(MT, P).T),
        "out_b": dram("out_b", a["L1_attn_out_b"]), "qkv_b": dram("qkv_b", a["L1_attn_qkv_b"]),
        "ffn_b": dram("ffn_b", a["L1_ffn_bias"]),
    }
    x = dram("x", a["x"].reshape(NB * S, H))
    ctxT = dram("ctxT", a["ctx_512"].transpose(2, 0, 1).reshape(CTX_L, NB * CTX_S))
    consts = dram("shape_constants", shape_constants())
    out = nc.dram_tensor("out", (NB * S, H), F32, kind="ExternalOutput").ap()
    build(nc, x, ctxT, consts, w, vec, out)
    r = run_bass_kernel_spmd(nc, [feed], core_ids=[0])
    return r.results[0]["out"].reshape(NB, S, H)
```

```python
from contextlib import ExitStack

import numpy as np
import concourse.bass as bass
from concourse import mybir

F32 = mybir.dt.float32
F32R = mybir.dt.float32r
FP8 = mybir.dt.float8e4
ALU = mybir.AluOpType
ACT = mybir.ActivationFunctionType
AX_X = mybir.AxisListType.X

P = 128
NB, S, H = 32, 32, 512
NH, HD = 16, 32
CTX_L, CTX_S = 128, 257
INNER = 1536
KT = H // P
TILES = NB * S // P
BPT = P // S
STAGES = ("x0", "a0", "f0", "x1", "a1", "f1")
ATTN = ("x0", "a0", "x1", "a1")
SOLVE_STEPS = 5
CHUNK = 2
MT = INNER // P
MASKED = -1e30
SCALE = float(1.0 / np.sqrt(np.float32(HD)))
EPS = 1e-5

C_IDENT, C_CAUSAL, C_STRICT, C_COS, C_SIN, C_REL, C_NOTFIRST, C_END = np.cumsum([0, P, S, S, HD, HD, S, 1])


def shape_constants():
    half = HD // 2
    c = np.zeros((P, C_END), np.float32)
    pos = np.arange(P) % S
    keys = np.arange(S)
    c[:, C_IDENT:C_CAUSAL] = np.eye(P)
    c[:, C_CAUSAL:C_STRICT] = np.where(keys[None] <= pos[:, None], 0.0, MASKED)
    c[:, C_STRICT:C_COS] = np.where(keys[None] < pos[:, None], 0.0, MASKED)
    inv_freq = np.float32(1.0) / np.float32(10000.0) ** (np.arange(half, dtype=np.float32) / np.float32(half))
    ang = pos.astype(np.float32)[:, None] * inv_freq[None]
    c[:, C_COS:C_SIN] = np.tile(np.cos(ang), (1, 2))
    c[:, C_SIN:C_REL] = np.concatenate([-np.sin(ang), np.sin(ang)], 1)
    c[:, C_REL:C_NOTFIRST] = (keys[None] - pos[:, None]).astype(np.float32)
    c[:, C_NOTFIRST] = pos > 0
    return c


SPLIT, QUANT, SIGN = "split", "quant", "sign"
UNITS = [("x0q", SPLIT, (0, 1)), ("x0kv", SPLIT, (2,)), ("x0o", SPLIT, (3, 4)),
         ("a0q", SPLIT, (5, 6)), ("a0k", SPLIT, (7, 8)), ("a0v", SPLIT, (9, 10)), ("a0o", SPLIT, (11, 12)),
         ("gate0", QUANT, (0,)), ("gate1", QUANT, (1,)), ("gate2", QUANT, (2,)),
         ("up0", QUANT, (3,)), ("up1", QUANT, (4,)), ("up2", QUANT, (13,)),
         ("down0", QUANT, (5,)), ("down1", QUANT, (6,)), ("down2", QUANT, (7,)),
         ("x1q", SPLIT, (8, 9)), ("x1kv", SPLIT, (10,)), ("x1o", SPLIT, (11, 12)),
         ("a1q", SPLIT, (0, 1)), ("a1k", SPLIT, (2, 3)), ("a1v", SPLIT, (4, 5)), ("a1o", SPLIT, (6, 7)),
         ("sign", SIGN, (13,))]
UNIT = {name: j for j, (name, _, _) in enumerate(UNITS)}
SLOTS = 14
FUSE_SLOTS = (10, 11, 12)
PREPARE_AT = {-4: ["x0q", "x0kv"], -1: ["x0o"], 1: ["a0q"], 2: ["a0k"], 3: ["a0v"], 4: ["a0o"],
              15: ["up2", "down0"],
              ("f0", 1): ["x1q"], ("f0", 3): ["x1kv", "x1o"],
              24: ["a1q"], 25: ["a1k"], 26: ["a1v"], 27: ["a1o"], 28: ["sign"]}
QUARTERS = 4
BESIDE_SOLVE = [(name, i) for name in ("gate0", "gate1", "gate2", "up0", "up1", "up2", "down0") for i in range(QUARTERS)]
BESIDE_SOLVE_FROM, BESIDE_SOLVE_PER_SLOT = 9, 4
HELD = ("up2", "down0")
BESIDE_F0 = [(name, i) for name in ("down1", "down2") for i in range(QUARTERS)]
BETA_AT = 0
ALPHA_AT = 29


def kind(g):
    return STAGES[g // TILES]


def attn_index(g):
    return sum(kind(i) in ATTN for i in range(g))


def stage_tiles(name):
    s = STAGES.index(name)
    return range(s * TILES, (s + 1) * TILES)


def build(nc, x, ctxT, consts, w, vec, out):
    with ExitStack() as es:
        def sb(name, shape, dt=F32):
            return es.enter_context(nc.sbuf_tensor(name, shape, dt))

        def sem(name):
            return es.enter_context(nc.semaphore(name))

        with nc.sbuf_tensor("lt_diag", [P, NH * P], F32) as lt_diag_mem:
            lt_diag = lt_diag_mem[:].rearrange("p (h c) -> p h c", h=NH)
        late_slot = sb("late_slot", [P, KT * 512], F32R)
        wt = sb("wt", [P, SLOTS - 1, KT * 512], F32R)
        raw = sb("raw", [P, 2, KT * 512])
        fp8 = sb("fp8", [P, 2, 512], FP8)
        xres = sb("xres", [P, TILES, H])
        cst = sb("cst", [P, int(C_END)])
        ones = sb("ones", [P, P])
        neg_half = sb("neg_half", [P, 1])
        scale_bc = sb("scale_bc", [P, H])
        bias_bc = sb("bias_bc", [P, 2, H])
        gu_scale = sb("gu_scale", [P, 2, MT])
        small_bc = sb("small_bc", [P, 2, NH])
        beta_raw = sb("beta_raw", [P, KT, NH])
        beta_w = sb("beta_w", [P, 2, KT, NH], F32R)
        stats = sb("stats", [P, 2, 6])
        mean_var = sb("mean_var", [P, 2, 2])
        norm = sb("norm", [P, 2, 3])
        xn = sb("xn", [P, 2, H])
        a_hi = sb("a_hi", [P, 2, KT, P], F32R)
        a_lo = sb("a_lo", [P, 2, KT, P], F32R)
        ctx_raw = sb("ctx_raw", [P, 2, P])
        ctx_hi = sb("ctx_hi", [P, 2, P], F32R)
        ctx_lo = sb("ctx_lo", [P, 2, P], F32R)
        q_sb = sb("q_sb", [P, H])
        k_sb = sb("k_sb", [P, H])
        rot = sb("rot", [P, H])
        qT = sb("qT", [P, H])
        kT = sb("kT", [P, H])
        v_sb = sb("v_sb", [P, 2, H])
        beta = sb("beta", [P, 2, NH])
        sc = sb("sc", [P, 2, H])
        ex = sb("ex", [P, 2, H])
        row_max = sb("row_max", [P, 2, NH])
        den = sb("den", [P, 2, NH])
        rden = sb("rden", [P, 2, NH])
        lrow = sb("lrow", [P, NH])
        pT = sb("pT", [P, H])
        o_sb = sb("o_sb", [P, H])
        o_hi = sb("o_hi", [P, KT, P], F32R)
        o_lo = sb("o_lo", [P, KT, P], F32R)
        solve = sb("solve", [P, 3 * H])
        LU = solve[:, 0:2 * H].rearrange("p (h c) -> p h c", h=NH)
        LT = solve[:, 2 * H:3 * H]

        def slot_mem(n):
            return wt[:, n, :] if n < SLOTS - 1 else late_slot[:]

        fuse = wt[:, FUSE_SLOTS[0]:FUSE_SLOTS[-1] + 1, :].rearrange(
            "p s n -> p (s n)").rearrange("p (a m t) -> p a m t", a=2, m=MT)

        ps = es.enter_context(nc.psum_tensor("ps", [P, 8, 512], F32))
        B_T, B_Q, B_K, B_V, B_S, B_KK, B_O, B_Y = range(8)
        B_KKS, B_QKS = B_S, B_S + 1
        GU_BANKS = (B_Q, B_K, B_V, B_O)

        x_loaded = [sem(f"x_loaded{i}") for i in range(2)]
        consts_loaded, bcast0_loaded = sem("consts_loaded"), sem("bcast0_loaded")
        f0_vec_loaded, a1_vec_loaded = sem("f0_vec_loaded"), sem("a1_vec_loaded")
        beta_raw_loaded = sem("beta_raw_loaded")
        raw_loaded = [sem(f"raw_loaded{i}") for i in range(2)]
        ctx_loaded = [sem(f"ctx_loaded{i}") for i in range(2)]
        pool_consts, pool_step, diag_zeroed = sem("pool_consts"), sem("pool_step"), sem("diag_zeroed")
        vec_step = sem("vec_step")
        w_hi, w_ready = sem("w_hi"), sem("w_ready")
        w_clipped, fp8_written, fp8_done, held_ready = (
            sem("w_clipped"), sem("fp8_written"), sem("fp8_done"), sem("held_ready"))
        sign_done, abs_done, alpha_mm, alpha_ready = sem("sign_done"), sem("abs_done"), sem("alpha_mm"), sem("alpha_ready")
        beta_hi, beta_w_ready = sem("beta_hi"), sem("beta_w_ready")
        stats_ready, rstd_ready, xn_ready = sem("stats_ready"), sem("rstd_ready"), sem("xn_ready")
        ln_T, a_hi_ready, a_ready = sem("ln_T"), sem("a_hi_ready"), sem("a_ready")
        ctx_hi_ready, ctx_ready = sem("ctx_hi_ready"), sem("ctx_ready")
        q_mm, k_mm, v_mm, beta_mm = sem("q_mm"), sem("k_mm"), sem("v_mm"), sem("beta_mm")
        qk_ready, v_ready, beta_ready = sem("qk_ready"), sem("v_ready"), sem("beta_ready")
        kk_mm, score_mm = sem("kk_mm"), sem("score_mm")
        kk_shifted, shifted, kk_exp, exp_done = sem("kk_shifted"), sem("shifted"), sem("kk_exp"), sem("exp_done")
        u0_ready, lt_ready, solve_mm, u_next, lk_ready, u_done = (
            sem("u0_ready"), sem("lt_ready"), sem("solve_mm"), sem("u_next"), sem("lk_ready"), sem("u_done"))
        p_ready, pv_mm, o_ready = sem("p_ready"), sem("pv_mm"), sem("o_ready")
        o_T, o_hi_ready, o_lo_ready, y_mm = sem("o_T"), sem("o_hi_ready"), sem("o_lo_ready"), sem("y_mm")
        x_new = sem("x_new")
        gu_mm, silu_ready, fused, fuse_hi, fuse_ready, down_mm = (
            sem("gu_mm"), sem("silu_ready"), sem("fused"), sem("fuse_hi"), sem("fuse_ready"), sem("down_mm"))
        sign_mm, stored = sem("sign_mm"), sem("stored")

        def quarter_of(unit_mem, i):
            return unit_mem[:, 512 * i:512 * (i + 1)]

        def heads(ap):
            return ap.rearrange("p (h c) -> p h c", h=NH)

        def per_head(ap):
            return ap.unsqueeze(2).broadcast_to([P, NH, S])

        def every_head(ap):
            return ap.unsqueeze(1).broadcast_to([P, NH, S])

        ident = cst[:, C_IDENT:C_CAUSAL]
        block = es.enter_context(nc.Block())

        A0 = stage_tiles("a0")
        RUN1, RUN2 = range(-3, 2 * TILES + 1), range(3 * TILES - 1, 6 * TILES + 1)

        def in_run(g, first=0):
            return 0 <= g < 6 * TILES and kind(g) != "f0"

        def is_attn(g):
            return in_run(g) and kind(g) in ATTN

        def a0_index(g):
            return g - A0[0]

        def attends_late(g):
            return is_attn(g) and kind(g) == "a0"

        def o_bank(g):
            return B_T if is_attn(g + 1) and kind(g + 1) == "a0" else B_KK

        def ctx_index(g):
            return g if kind(g) == "x0" else TILES + g - stage_tiles("x1")[0]

        def ctx_tile(n):
            return n if n < TILES else stage_tiles("x1")[0] + n - TILES

        def normalised_here(g):
            return 0 <= g + 3 <= 2 * TILES + 2 or 3 * TILES + 2 <= g + 3 < 6 * TILES

        def transposed_here(g):
            return 0 <= g + 2 < 2 * TILES + CHUNK or 3 * TILES + CHUNK <= g + 2 < 6 * TILES

        def f0_normalised(c):
            return [g for g in range(2 * TILES + CHUNK * (c + 1), 2 * TILES + CHUNK * (c + 2)) if g > 2 * TILES + 2]

        def a_free(eng, g):
            if g < 2:
                return
            k = kind(g - 2)
            if k in ATTN:
                eng.wait_ge(v_mm, attn_index(g - 2) + 1)
                if k == "a0":
                    eng.wait_ge(beta_mm, a0_index(g - 2) + 1)
            elif k == "f0":
                eng.wait_ge(gu_mm, MT * ((g - 2 - 2 * TILES) // CHUNK + 1))
            else:
                eng.wait_ge(sign_mm, g - 2 - stage_tiles("f1")[0] + 1)

        def quarters_of_slot(g, nth):
            n = BESIDE_SOLVE_PER_SLOT * (g - BESIDE_SOLVE_FROM) + nth
            return BESIDE_SOLVE[n:n + 1] if n >= 0 else ()

        def slots_free(eng, name):
            stage = name[:2]
            if name[:4] == "gate" or name in ("up0", "up1"):
                eng.wait_ge(v_mm, TILES)
                eng.wait_ge(y_mm, TILES)
            elif name[:4] == "down" or name == "x1q":
                eng.wait_ge(v_mm, 2 * TILES)
            elif name == "up2":
                eng.wait_ge(u_done, 2 * TILES)
            elif name in ("x1kv", "x1o"):
                eng.wait_ge(down_mm, TILES)
            elif stage == "a1" or name == "sign":
                eng.wait_ge(gu_mm, MT * TILES // CHUNK)
                eng.wait_ge(down_mm, TILES)

        HALVES = (slice(0, NH // 2), slice(NH // 2, NH))
        solve_out = ps[:, B_KKS:B_KKS + 2, :].rearrange("p b n -> p (b n)").rearrange("p (h c) -> p h c", h=NH)

        def quarter_mem(name, i):
            j, cols = UNIT[name], slice(512 * i, 512 * (i + 1))
            return raw[:, j % 2, cols], slot_mem(UNITS[j][2][0])[:, cols]

        def clipped_of(q):
            return bias_bc[:, q % 2, :]

        @block.sync
        def _(sp):
            xv = x.rearrange("(t p) d -> p t d", p=P)
            sp.dma_start(xres[:, 0:1, :], xv[:, 0:1, :]).then_inc(x_loaded[0], 16)
            sp.dma_start(cst[:], consts).then_inc(consts_loaded, 16)

            def load_unit(j):
                name, how, slots = UNITS[j]
                if j >= 2:
                    sp.wait_ge(w_ready, j - 1)
                dst = raw[:, j % 2, :]
                if name.endswith("kv"):
                    dst = dst[:, 0:1024]
                else:
                    dst = dst.rearrange("p (k n) -> p k n", k=KT)
                sp.dma_start(dst, w[name]).then_inc(raw_loaded[j % 2], 16)

            load_unit(0)
            load_unit(1)
            sp.dma_start(xres[:, 1:TILES, :], xv[:, 1:TILES, :]).then_inc(x_loaded[1], 16)
            sp.dma_start(beta_raw[:], vec["Wb"].rearrange("(k p) n -> p k n", p=P)).then_inc(beta_raw_loaded, 16)
            sp.dma_start(small_bc[:, 0, :], vec["bb"].partition_broadcast(P)).then_inc(bcast0_loaded, 16)
            sp.dma_start(small_bc[:, 1, :], vec["slopes"].partition_broadcast(P)).then_inc(bcast0_loaded, 16)
            sp.dma_start(scale_bc[:], vec["down_scale"].partition_broadcast(P)).then_inc(f0_vec_loaded, 16)
            sp.dma_start(gu_scale[:, 0, :], vec["gate_scale"]).then_inc(f0_vec_loaded, 16)
            sp.dma_start(gu_scale[:, 1, :], vec["up_scale"]).then_inc(f0_vec_loaded, 16)
            for j in range(2, UNIT["a1q"]):
                load_unit(j)
            sp.wait_ge(pv_mm, 2 * TILES)
            sp.dma_start(solve[:], vec["qkv_b"].partition_broadcast(P)).then_inc(a1_vec_loaded, 16)
            sp.wait_ge(w_ready, UNIT["down2"] + 1)
            sp.dma_start(bias_bc[:, 0, :], vec["out_b"].partition_broadcast(P)).then_inc(a1_vec_loaded, 16)
            sp.dma_start(bias_bc[:, 1, :], vec["ffn_b"].partition_broadcast(P)).then_inc(a1_vec_loaded, 16)
            for j in range(UNIT["a1q"], len(UNITS)):
                load_unit(j)
            ov = out.rearrange("(t p) d -> p t d", p=P)
            for g in stage_tiles("f1"):
                sp.wait_ge(x_new, g + 1)
                sp.dma_start(ov[:, g % TILES, :], xres[:, g % TILES, :]).then_inc(stored, 16)
            sp.wait_ge(stored, 16 * TILES)

        @block.gpsimd
        def _(pool):
            steps = 0
            nc.gpsimd.memset(neg_half[:], -0.5).then_inc(pool_consts, 1)
            nc.gpsimd.memset(ones[:], 1.0).then_inc(pool_consts, 1)
            nc.gpsimd.memset(lt_diag[:], 0.0).then_inc(diag_zeroed, 1)
            ctx_view = ctxT.rearrange("l (b k) -> l b k", k=CTX_S)

            def load_ctx(n):
                t = n % TILES
                if n >= 2:
                    pool.wait_ge(ctx_ready, n - 1)
                pool.dma_start(ctx_raw[:, n % 2, :].rearrange("p (b k) -> p b k", b=BPT),
                               ctx_view[:, BPT * t:BPT * (t + 1), 0:S]).then_inc(ctx_loaded[n % 2], 16)

            load_ctx(0)
            load_ctx(1)
            pool.wait_ge(pool_consts, 2)
            for g in range(6 * TILES):
                b = g % 2
                pool.wait_ge(stats_ready, g + 1)
                if g >= 2:
                    pool.wait_ge(xn_ready, g - 1)
                nc.gpsimd.tensor_scalar(norm[:, b, 0:1], mean_var[:, b, 1:2], EPS, None, ALU.add).then_inc(pool_step, 1)
                steps += 1
                pool.wait_ge(pool_step, steps)
                nc.gpsimd.tensor_tensor(norm[:, b, 1:2], norm[:, b, 0:1], neg_half[:], ALU.pow).then_inc(pool_step, 1)
                steps += 1
                pool.wait_ge(pool_step, steps)
                nc.gpsimd.tensor_scalar(norm[:, b, 2:3], mean_var[:, b, 0:1], -1.0, norm[:, b, 1:2],
                                        ALU.mult, ALU.mult).then_inc(rstd_ready, 1)
                for n in range(2, 2 * TILES):
                    if g == (n + 2 if n in (TILES, TILES + 1) else ctx_tile(n)):
                        load_ctx(n)

        @block.scalar
        def _(act):
            split_jobs = [0]
            quarters = [0]
            ctx_tiles = [0]

            def quant_quarter(name, i):
                x, near = quarter_of(raw[:, UNIT[name] % 2, :], i), clipped_of(quarters[0])
                quarters[0] += 1
                if quarters[0] > 1:
                    act.wait_ge(fp8_done, quarters[0] - 1)
                act.wait_ge(w_clipped, quarters[0])
                nc.scalar.activation(fp8[:, 0, :], near, ACT.Copy, saturate=False)
                nc.scalar.activation(fp8[:, 1, :], x, ACT.Copy, scale=0.25, saturate=False).then_inc(fp8_written, 1)
                act.wait_ge(fp8_written, quarters[0])
                nc.scalar.activation(near, fp8[:, 0, :], ACT.Copy)
                nc.scalar.activation(x, fp8[:, 1, :], ACT.Copy, scale=4.0).then_inc(fp8_done, 1)

            def quarter_beside_solve(g, nth):
                for name, i in quarters_of_slot(g, nth):
                    quant_quarter(name, i)

            def prepare(name):
                j = UNIT[name]
                _, how, slots = UNITS[j]
                if how != QUANT:
                    act.wait_ge(raw_loaded[j % 2], 16 * (j // 2 + 1))
                slots_free(act, name)
                r = raw[:, j % 2, :]
                if how == SPLIT:
                    if name.endswith("kv"):
                        dst, r = slot_mem(slots[0])[:, 0:1024], r[:, 0:1024]
                    else:
                        dst = slot_mem(slots[0])
                    nc.scalar.activation(dst, r, ACT.Copy).then_inc(w_hi, 1)
                elif how == QUANT:
                    act.wait_ge(held_ready, HELD.index(name) + 1)
                    nc.scalar.activation(slot_mem(slots[0]), r, ACT.Copy).then_inc(w_ready, 1)
                else:
                    act.wait_ge(sign_done, 1)
                    nc.scalar.activation(r, r, ACT.Abs).then_inc(abs_done, 1)

            def normalise(g):
                act.wait_ge(rstd_ready, g + 1)
                if g >= 2:
                    act.wait_ge(ln_T, g - 1)
                nc.scalar.activation(xn[:, g % 2, :], xres[:, g % TILES, :], ACT.Identity,
                                     scale=norm[:, g % 2, 1:2], bias=norm[:, g % 2, 2:3]).then_inc(xn_ready, 1)

            def split_a(g):
                act.wait_ge(ln_T, g + 1)
                a_free(act, g)
                nc.scalar.activation(a_hi[:, g % 2, :, :], ps[:, B_T, :].rearrange("p (k t) -> p k t", k=KT),
                                     ACT.Copy).then_inc(a_hi_ready, 1)

            def split_ctx(g):
                n = ctx_tiles[0]
                ctx_tiles[0] += 1
                act.wait_ge(ctx_loaded[n % 2], 16 * (n // 2 + 1))
                if n >= 2:
                    act.wait_ge(v_mm, attn_index(ctx_tile(n - 2)) + 1)
                nc.scalar.activation(ctx_hi[:, n % 2, :], ctx_raw[:, n % 2, :], ACT.Copy).then_inc(ctx_hi_ready, 1)

            def exponentials(g):
                act.wait_ge(shifted, attn_index(g) + 1)
                nc.scalar.activation(ex[:, 0, :], sc[:, 0, :], ACT.Exp).then_inc(exp_done, 1)

            def split_o(g):
                if is_attn(g):
                    a = attn_index(g)
                    act.wait_ge(o_T, a + 1)
                    if a:
                        act.wait_ge(y_mm, a)
                    nc.scalar.activation(o_hi[:], ps[:, o_bank(g), :].rearrange("p (k t) -> p k t", k=KT),
                                         ACT.Copy).then_inc(o_hi_ready, 1)

            def take_v(g):
                if not is_attn(g) or kind(g) == "a1":
                    return
                a = attn_index(g)
                act.wait_ge(v_mm, a + 1)
                if a >= 2:
                    act.wait_ge(pv_mm, a - 1)
                if a >= TILES + 2:
                    act.wait_ge(u0_ready, min(a - 1 - TILES, TILES))
                nc.scalar.activation(v_sb[:, g % 2, :], ps[:, B_V, :], ACT.Copy).then_inc(v_ready, 1)

            def take_a(g):
                if transposed_here(g - 2):
                    if kind(g)[0] == "x":
                        split_ctx(g)
                    split_a(g)

            def spread_lt(hs):
                for b in range(BPT):
                    rows = slice(S * b, S * (b + 1))
                    last = nc.scalar.activation(lt_diag[rows, hs, rows], heads(LT)[rows, hs, :], ACT.Copy)
                last.then_inc(lk_ready, 1)

            def next_lk(g, s):
                for half, hs in enumerate(HALVES):
                    act.wait_ge(u_next, 2 * (a0_index(g) * (SOLVE_STEPS - 1) + s) + half + 1)
                    nc.scalar.activation(LU[:, hs, 0:S], solve_out[:, hs, 0:S], ACT.Copy)
                    spread_lt(hs)

            def a0_slot(g):
                a = attn_index(g)
                quarter_beside_solve(g, 0)
                act.wait_ge(kk_shifted, a0_index(g) + 1)
                nc.scalar.activation(ex[:, 1, :], sc[:, 1, :], ACT.Exp).then_inc(kk_exp, 1)
                act.wait_ge(v_ready, a + 1)
                act.wait_ge(pv_mm, a)
                nc.scalar.activation(LU[:, :, S:2 * S], heads(v_sb[:, g % 2, :]), ACT.Copy).then_inc(u0_ready, 1)
                for half, hs in enumerate(HALVES):
                    act.wait_ge(lt_ready, 2 * a0_index(g) + half + 1)
                    act.wait_ge(diag_zeroed, 1)
                    spread_lt(hs)
                split_o(g - 1)
                if normalised_here(g):
                    normalise(g + 3)
                quarter_beside_solve(g, 1)
                next_lk(g, 0)
                next_lk(g, 1)
                exponentials(g)
                quarter_beside_solve(g, 2)
                next_lk(g, 2)
                take_a(g + 2)
                take_v(g + 1)
                quarter_beside_solve(g, 3)

            def slot(g):
                if is_attn(g):
                    exponentials(g)
                split_o(g - 1)
                if normalised_here(g):
                    normalise(g + 3)
                take_v(g + 1)
                take_a(g + 2)

            for name in PREPARE_AT[-4]:
                prepare(name)
            for g in RUN1:
                a0_slot(g) if g in A0 else slot(g)
                if g == BETA_AT:
                    act.wait_ge(beta_raw_loaded, 16)
                    nc.scalar.activation(beta_w[:, 0], beta_raw[:], ACT.Copy).then_inc(beta_hi, 1)
                for name in PREPARE_AT.get(g, ()):
                    prepare(name)
            act.wait_ge(f0_vec_loaded, 48)
            for c in range(TILES // CHUNK):
                for g in f0_normalised(c):
                    normalise(g)
                for m in range(MT + 1):
                    n = c * MT + m
                    if m < MT:
                        act.wait_ge(gu_mm, n + 1)
                        if n >= 2:
                            act.wait_ge(fused, n - 1)
                        nc.scalar.activation(ex[:, m % 2, 0:CHUNK * P], ps[:, GU_BANKS[n % 4], 0:CHUNK * P], ACT.Silu,
                                             scale=gu_scale[:, 0, m:m + 1]).then_inc(silu_ready, 1)
                    if m:
                        act.wait_ge(fused, n)
                        if m == 1:
                            act.wait_ge(y_mm, 2 * TILES)
                            if c:
                                act.wait_ge(down_mm, CHUNK * c)
                        nc.scalar.activation(fuse[:, 0, m - 1, :], sc[:, (m - 1) % 2, 0:CHUNK * P],
                                             ACT.Copy).then_inc(fuse_hi, 1)
                    if c == 0 and 1 <= m <= len(BESIDE_F0):
                        quant_quarter(*BESIDE_F0[m - 1])
                for i in range(CHUNK):
                    g = 2 * TILES + CHUNK * (c + 1) + i
                    if kind(g)[0] == "x":
                        split_ctx(g)
                    split_a(g)
                for name in PREPARE_AT.get(("f0", c), ()):
                    prepare(name)
            for g in RUN2:
                slot(g)
                for name in PREPARE_AT.get(g, ()):
                    prepare(name)

        @block.vector
        def _(dve):
            steps = [0]
            splits = [0]
            ctx_tiles = [0]

            def step(ins):
                ins.then_inc(vec_step, 1)
                steps[0] += 1
                dve.wait_ge(vec_step, steps[0])

            def clip_quarter(q, name, i):
                j = UNIT[name]
                if i == 0:
                    dve.wait_ge(raw_loaded[j % 2], 16 * (j // 2 + 1))
                nc.vector.tensor_scalar(clipped_of(q), quarter_of(raw[:, j % 2, :], i), 240.0, -240.0,
                                        ALU.min, ALU.max).then_inc(w_clipped, 1)

            def add_quarter(q, name, i):
                j = UNIT[name]
                x, near = quarter_of(raw[:, j % 2, :], i), clipped_of(q)
                dve.wait_ge(fp8_done, q + 1)
                step(nc.vector.scalar_tensor_tensor(out=near, in0=x, scalar=240.0, in1=near, op0=ALU.max, op1=ALU.add))
                if name in HELD:
                    out, done, count = x, held_ready, HELD.index(name)
                else:
                    out, done, count = quarter_of(slot_mem(UNITS[j][2][0]), i), w_ready, j
                    if i == 0:
                        slots_free(dve, name)
                        dve.wait_ge(w_ready, j)
                last = nc.vector.scalar_tensor_tensor(out=out, in0=x, scalar=-240.0, in1=near, op0=ALU.min, op1=ALU.add)
                if i == QUARTERS - 1:
                    last.then_inc(done, 1)
                    dve.wait_ge(done, count + 1)
                else:
                    step(last)

            def quarter_beside_solve(g, nth):
                q = BESIDE_SOLVE_PER_SLOT * (g - BESIDE_SOLVE_FROM) + nth
                for name, i in quarters_of_slot(g, nth):
                    add_quarter(q, name, i)
                    if q + 1 < len(BESIDE_SOLVE):
                        clip_quarter(q + 1, *BESIDE_SOLVE[q + 1])

            def prepare(name):
                j = UNIT[name]
                _, how, slots = UNITS[j]
                r = raw[:, j % 2, :]
                if how == SPLIT:
                    splits[0] += 1
                    dve.wait_ge(w_hi, splits[0])
                    if name.endswith("kv"):
                        hi, lo, r = slot_mem(slots[0])[:, 0:1024], slot_mem(slots[0])[:, 1024:2048], r[:, 0:1024]
                    else:
                        hi, lo = slot_mem(slots[0]), slot_mem(slots[1])
                    nc.vector.tensor_tensor(lo, r, hi.bitcast(F32), ALU.subtract).then_inc(w_ready, 1)
                elif how == SIGN:
                    dve.wait_ge(raw_loaded[j % 2], 16 * (j // 2 + 1))
                    slots_free(dve, name)
                    dst = slot_mem(slots[0])
                    step(nc.vector.tensor_scalar(dst, r, 0.0, 2.0, ALU.is_ge, ALU.mult))
                    nc.vector.tensor_scalar(dst, dst.bitcast(F32), -1.0, None, ALU.add).then_inc(sign_done, 1)

            def ln_stats(g):
                if g < TILES:
                    dve.wait_ge(x_loaded[min(g, 1)], 16)
                else:
                    dve.wait_ge(x_new, g - TILES + 1)
                if g >= 2:
                    dve.wait_ge(rstd_ready, g - 1)
                step(nc.vector.bn_stats(stats[:, g % 2, :], xres[:, g % TILES, :]))
                nc.vector.bn_aggr(mean_var[:, g % 2, :], stats[:, g % 2, :]).then_inc(stats_ready, 1)

            def split_a(g):
                dve.wait_ge(a_hi_ready, g + 1)
                nc.vector.tensor_tensor(a_lo[:, g % 2, :, :], ps[:, B_T, :].rearrange("p (k t) -> p k t", k=KT),
                                        a_hi[:, g % 2, :, :].bitcast(F32), ALU.subtract).then_inc(a_ready, 1)

            def split_ctx(g):
                n = ctx_tiles[0]
                ctx_tiles[0] += 1
                dve.wait_ge(ctx_hi_ready, n + 1)
                nc.vector.tensor_tensor(ctx_lo[:, n % 2, :], ctx_raw[:, n % 2, :], ctx_hi[:, n % 2, :].bitcast(F32),
                                        ALU.subtract).then_inc(ctx_ready, 1)

            def softmax_shift(bank, buf, mask, done):
                in1 = heads(rot[:]) if mask is None else every_head(mask)
                step(nc.vector.scalar_tensor_tensor(out=heads(sc[:, buf, :]), in0=heads(ps[:, bank, :]), scalar=SCALE,
                                                    in1=in1, op0=ALU.mult, op1=ALU.add))
                step(nc.vector.tensor_reduce(row_max[:, buf, :], heads(sc[:, buf, :]), AX_X, ALU.max))
                nc.vector.tensor_tensor(heads(sc[:, buf, :]), heads(sc[:, buf, :]), per_head(row_max[:, buf, :]),
                                        ALU.subtract).then_inc(done, 1)

            def rope(bank, dst):
                src = ps[:, bank, :].rearrange("p (h a c) -> p h a c", h=NH, a=2)
                halves = rot[:].rearrange("p (h a c) -> p h a c", h=NH, a=2)
                half = HD // 2
                nc.vector.tensor_tensor(heads(dst), heads(ps[:, bank, :]), every_head(cst[:, C_COS:C_SIN]), ALU.mult)
                for a in range(2):
                    sin = cst[:, C_SIN + half * a:C_SIN + half * (a + 1)]
                    last = nc.vector.tensor_tensor(halves[:, :, a, :], src[:, :, 1 - a, :],
                                                   sin.unsqueeze(1).broadcast_to([P, NH, half]), ALU.mult)
                step(last)
                step(nc.vector.tensor_tensor(dst, dst, rot[:], ALU.add))

            def rotate_q(g):
                if is_attn(g) and kind(g) == "a0":
                    dve.wait_ge(q_mm, attn_index(g) + 1)
                    rope(B_Q, q_sb[:])

            def take_q(g):
                if not is_attn(g):
                    return
                a = attn_index(g)
                dve.wait_ge(q_mm, a + 1)
                if kind(g) == "a1":
                    step(nc.vector.tensor_tensor(q_sb[:], ps[:, B_Q, :], solve[:, 0:H], ALU.add))
                if a:
                    dve.wait_ge(score_mm, a)
                step(nc.vector.transpose(qT[:], ps[:, B_Q, :] if kind(g)[0] == "x" else q_sb[:]))

            def rotate_k(g):
                if is_attn(g) and kind(g) == "a0":
                    dve.wait_ge(k_mm, attn_index(g) + 1)
                    rope(B_K, k_sb[:])

            def take_k(g):
                if not is_attn(g):
                    return
                dve.wait_ge(k_mm, attn_index(g) + 1)
                if kind(g) == "a1":
                    step(nc.vector.tensor_tensor(k_sb[:], ps[:, B_K, :], solve[:, H:2 * H], ALU.add))
                nc.vector.transpose(kT[:], ps[:, B_K, :] if kind(g)[0] == "x" else k_sb[:]).then_inc(qk_ready, 1)

            def take_rest(g):
                if not in_run(g):
                    return
                if kind(g) == "a0":
                    n = a0_index(g)
                    dve.wait_ge(beta_mm, n + 1)
                    nc.vector.tensor_tensor(beta[:, g % 2, :], ps[:, B_O, 0:NH], small_bc[:, 0, :],
                                            ALU.add).then_inc(beta_ready, 1)
                elif kind(g) == "a1":
                    a = attn_index(g)
                    dve.wait_ge(v_mm, a + 1)
                    dve.wait_ge(pv_mm, a - 1)
                    nc.vector.tensor_tensor(v_sb[:, g % 2, :], ps[:, B_V, :], solve[:, 2 * H:3 * H],
                                            ALU.add).then_inc(v_ready, 1)

            def take_sign(g):
                if in_run(g) and kind(g) == "f1":
                    n = g - stage_tiles("f1")[0]
                    if n == 0:
                        dve.wait_ge(alpha_ready, 1)
                    dve.wait_ge(sign_mm, n + 1)
                    step(nc.vector.tensor_tensor(k_sb[:], ps[:, B_Q + g % 2, :], scale_bc[:], ALU.mult))
                    step(nc.vector.tensor_tensor(k_sb[:], k_sb[:], bias_bc[:, 1, :], ALU.add))
                    nc.vector.tensor_tensor(xres[:, g % TILES, :], xres[:, g % TILES, :], k_sb[:],
                                            ALU.add).then_inc(x_new, 1)
                    dve.wait_ge(x_new, g + 1)

            def residual(g):
                if not is_attn(g):
                    return
                t = g % TILES
                dve.wait_ge(y_mm, attn_index(g) + 1)
                if kind(g) == "a1":
                    step(nc.vector.tensor_tensor(xres[:, t, :], xres[:, t, :], bias_bc[:, 0, :], ALU.add))
                nc.vector.tensor_tensor(xres[:, t, :], xres[:, t, :], ps[:, B_Y, :], ALU.add).then_inc(x_new, 1)

            def take_a(g):
                if transposed_here(g - 2):
                    if kind(g)[0] == "x":
                        split_ctx(g)
                    split_a(g)

            def stats_next(g):
                if normalised_here(g):
                    ln_stats(g + 3)

            def o_norm(g):
                if is_attn(g):
                    a = attn_index(g)
                    dve.wait_ge(pv_mm, a + 1)
                    if a:
                        dve.wait_ge(o_T, a)
                    nc.vector.tensor_tensor(heads(o_sb[:]), heads(ps[:, B_O, :]), per_head(rden[:, 0, :]),
                                            ALU.mult).then_inc(o_ready, 1)

            def split_o(g):
                if is_attn(g):
                    dve.wait_ge(o_hi_ready, attn_index(g) + 1)
                    nc.vector.tensor_tensor(o_lo[:], ps[:, o_bank(g), :].rearrange("p (k t) -> p k t", k=KT),
                                            o_hi[:].bitcast(F32), ALU.subtract).then_inc(o_lo_ready, 1)

            def causal_shift(g):
                dve.wait_ge(score_mm, attn_index(g) + 1)
                softmax_shift(B_V if kind(g) == "a0" else B_S, 0, cst[:, C_CAUSAL:C_STRICT], shifted)

            def alibi_shift(g):
                if g == stage_tiles("a1")[0]:
                    for h in range(NH):
                        last = nc.vector.scalar_tensor_tensor(
                            out=rot[:, S * h:S * (h + 1)], in0=cst[:, C_REL:C_NOTFIRST], scalar=small_bc[:, 1, h:h + 1],
                            in1=cst[:, C_CAUSAL:C_STRICT], op0=ALU.mult, op1=ALU.add)
                    step(last)
                dve.wait_ge(score_mm, attn_index(g) + 1)
                softmax_shift(B_S, 0, None, shifted)

            def transpose_p(g):
                a = attn_index(g)
                dve.wait_ge(exp_done, a + 1)
                if a:
                    dve.wait_ge(pv_mm, a)
                nc.vector.transpose(pT[:], ex[:, 0, :]).then_inc(p_ready, 1)
                step(nc.vector.tensor_reduce(den[:, 0, :], heads(ex[:, 0, :]), AX_X, ALU.add))
                step(nc.vector.reciprocal(rden[:, 0, :], den[:, 0, :]))

            def make_l(g):
                n = a0_index(g)
                dve.wait_ge(kk_mm, n + 1)
                softmax_shift(B_S, 1, cst[:, C_STRICT:C_COS], kk_shifted)
                dve.wait_ge(kk_exp, n + 1)
                step(nc.vector.tensor_reduce(den[:, 1, :], heads(ex[:, 1, :]), AX_X, ALU.add))
                step(nc.vector.reciprocal(rden[:, 1, :], den[:, 1, :]))
                dve.wait_ge(beta_ready, n + 1)
                step(nc.vector.scalar_tensor_tensor(out=lrow[:], in0=rden[:, 1, :], scalar=cst[:, C_NOTFIRST:C_END],
                                                    in1=beta[:, g % 2, :], op0=ALU.mult, op1=ALU.mult))
                step(nc.vector.tensor_tensor(LU[:, :, 0:S], heads(ex[:, 1, :]), per_head(lrow[:]), ALU.mult))
                for hs in HALVES:
                    nc.vector.transpose(heads(LT)[:, hs, :], LU[:, hs, 0:S]).then_inc(lt_ready, 1)

            def solve_step(g, s):
                last = s == SOLVE_STEPS - 1
                for half, hs in enumerate(HALVES):
                    dve.wait_ge(solve_mm, 2 * (a0_index(g) * SOLVE_STEPS + s) + half + 1)
                    if not last:
                        nc.vector.transpose(heads(LT)[:, hs, :], solve_out[:, hs, 0:S])
                    nc.vector.tensor_tensor(LU[:, hs, S:2 * S], LU[:, hs, S:2 * S], solve_out[:, hs, S:2 * S],
                                            ALU.subtract if s == 0 else ALU.add).then_inc(u_done if last else u_next, 1)

            def a0_slot(g):
                if g == BESIDE_SOLVE_FROM:
                    clip_quarter(0, *BESIDE_SOLVE[0])
                make_l(g)
                o_norm(g - 1)
                stats_next(g)
                split_o(g - 1)
                quarter_beside_solve(g, 0)
                solve_step(g, 0)
                take_rest(g + 1)
                rotate_q(g + 1)
                quarter_beside_solve(g, 1)
                solve_step(g, 1)
                causal_shift(g)
                solve_step(g, 2)
                take_q(g + 1)
                rotate_k(g + 1)
                solve_step(g, 3)
                take_k(g + 1)
                take_a(g + 2)
                residual(g - 1)
                quarter_beside_solve(g, 2)
                solve_step(g, 4)
                transpose_p(g)
                quarter_beside_solve(g, 3)

            def slot(g):
                o_norm(g - 1)
                if is_attn(g):
                    alibi_shift(g) if kind(g) == "a1" else causal_shift(g)
                split_o(g - 1)
                if is_attn(g):
                    transpose_p(g)
                stats_next(g)
                rotate_q(g + 1)
                take_q(g + 1)
                rotate_k(g + 1)
                take_k(g + 1)
                take_rest(g + 1)
                take_a(g + 2)
                residual(g - 1)
                take_sign(g)

            for name in PREPARE_AT[-4]:
                prepare(name)
            dve.wait_ge(consts_loaded, 16)
            dve.wait_ge(bcast0_loaded, 32)
            for g in RUN1:
                a0_slot(g) if g in A0 else slot(g)
                if g == BETA_AT:
                    dve.wait_ge(beta_hi, 1)
                    nc.vector.tensor_tensor(beta_w[:, 1], beta_raw[:], beta_w[:, 0].bitcast(F32),
                                            ALU.subtract).then_inc(beta_w_ready, 1)
                for name in PREPARE_AT.get(g, ()):
                    prepare(name)
            dve.wait_ge(f0_vec_loaded, 48)
            for c in range(TILES // CHUNK):
                for g in f0_normalised(c):
                    ln_stats(g)
                for m in range(MT + 1):
                    n = c * MT + m
                    if m < MT:
                        dve.wait_ge(silu_ready, n + 1)
                        if n >= 2:
                            dve.wait_ge(fuse_hi, n - 1)
                            dve.wait_ge(fuse_ready, n - 1)
                        nc.vector.scalar_tensor_tensor(
                            out=sc[:, m % 2, 0:CHUNK * P], in0=ps[:, GU_BANKS[n % 4], CHUNK * P:2 * CHUNK * P],
                            scalar=gu_scale[:, 1, m:m + 1], in1=ex[:, m % 2, 0:CHUNK * P], op0=ALU.mult,
                            op1=ALU.mult).then_inc(fused, 1)
                    if m:
                        dve.wait_ge(fuse_hi, n)
                        nc.vector.tensor_tensor(fuse[:, 1, m - 1, :], sc[:, (m - 1) % 2, 0:CHUNK * P],
                                                fuse[:, 0, m - 1, :].bitcast(F32), ALU.subtract).then_inc(fuse_ready, 1)
                    if c == 0 and 2 <= m < len(BESIDE_F0) + 2:
                        add_quarter(len(BESIDE_SOLVE) + m - 2, *BESIDE_F0[m - 2])
                    if c == 0 and m < len(BESIDE_F0):
                        clip_quarter(len(BESIDE_SOLVE) + m, *BESIDE_F0[m])
                for i in range(CHUNK):
                    g = 2 * TILES + CHUNK * (c + 1) + i
                    if kind(g)[0] == "x":
                        split_ctx(g)
                    split_a(g)
                for i in range(CHUNK):
                    g = 2 * TILES + CHUNK * c + i
                    dve.wait_ge(down_mm, CHUNK * c + i + 1)
                    step(nc.vector.tensor_tensor(k_sb[:], ps[:, B_S + i, :], scale_bc[:], ALU.mult))
                    nc.vector.tensor_tensor(xres[:, g % TILES, :], xres[:, g % TILES, :], k_sb[:],
                                            ALU.add).then_inc(x_new, 1)
                    dve.wait_ge(x_new, g + 1)
                for name in PREPARE_AT.get(("f0", c), ()):
                    prepare(name)
            dve.wait_ge(a1_vec_loaded, 48)
            for g in RUN2:
                slot(g)
                for name in PREPARE_AT.get(g, ()):
                    prepare(name)
                if g == ALPHA_AT:
                    dve.wait_ge(alpha_mm, 1)
                    nc.vector.tensor_scalar(scale_bc[:], ps[:, B_Y, :], 1.0 / H, None, ALU.mult).then_inc(alpha_ready, 1)

        @block.tensor
        def _(pe):
            issued = {"ln_T": 0, "o_T": 0}

            def mm3(dst, hi, lo, w_hi_of, w_lo_of, nk, done):
                for k in range(nk):
                    nc.tensor.matmul(dst, hi(k), w_hi_of(k), start=(k == 0), stop=False)
                    yield
                    nc.tensor.matmul(dst, hi(k), w_lo_of(k), start=False, stop=False)
                    yield
                    last = nc.tensor.matmul(dst, lo(k), w_hi_of(k), start=False, stop=(k == nk - 1))
                    if k == nk - 1:
                        last.then_inc(done, 1)
                    yield

            def issue(products, n=None):
                for i, _ in enumerate(products):
                    if i + 1 == n:
                        break

            def weight(slot, k):
                return slot_mem(slot)[:, 512 * k:512 * (k + 1)]

            def bank_T_free():
                if issued["ln_T"]:
                    pe.wait_ge(a_ready, issued["ln_T"])
                if issued["o_T"]:
                    pe.wait_ge(o_lo_ready, issued["o_T"])

            def ln_transpose(g):
                pe.wait_ge(xn_ready, g + 1)
                bank_T_free()
                for k in range(KT):
                    last = nc.tensor.transpose(ps[:, B_T, P * k:P * (k + 1)], xn[:, g % 2, P * k:P * (k + 1)], ident)
                last.then_inc(ln_T, 1)
                issued["ln_T"] += 1

            def project(name, g, bank, done):
                hi_slot, lo_slot = UNITS[UNIT[name]][2]
                pe.wait_ge(w_ready, UNIT[name] + 1)
                pe.wait_ge(a_ready, g + 1)
                yield from mm3(ps[:, bank, :], lambda k: a_hi[:, g % 2, k, :], lambda k: a_lo[:, g % 2, k, :],
                               lambda k: weight(hi_slot, k), lambda k: weight(lo_slot, k), KT, done)

            def q_project(g):
                if not is_attn(g):
                    return
                a = attn_index(g)
                if a:
                    pe.wait_ge(qk_ready, a)
                if a == 2 * TILES:
                    pe.wait_ge(fused, MT * TILES // CHUNK)
                yield from project(kind(g) + "q", g, B_Q, q_mm)

            def k_project(g):
                if not is_attn(g):
                    return
                if kind(g)[0] == "x":
                    n = ctx_index(g)
                    pe.wait_ge(ctx_ready, n + 1)
                    pe.wait_ge(w_ready, UNIT[kind(g) + "kv"] + 1)
                    slot, b = UNITS[UNIT[kind(g) + "kv"]][2][0], n % 2
                    yield from mm3(ps[:, B_K, :], lambda k: ctx_hi[:, b, :], lambda k: ctx_lo[:, b, :],
                                   lambda k: slot_mem(slot)[:, 0:512], lambda k: slot_mem(slot)[:, 1024:1536], 1, k_mm)
                else:
                    yield from project(kind(g) + "k", g, B_K, k_mm)

            def v_project(g):
                if not is_attn(g):
                    return
                a = attn_index(g)
                if a:
                    pe.wait_ge(v_ready, a)
                if is_attn(g - 1) and kind(g - 1) == "a0":
                    pe.wait_ge(shifted, a)
                if kind(g)[0] == "x":
                    b = ctx_index(g) % 2
                    slot = UNITS[UNIT[kind(g) + "kv"]][2][0]
                    yield from mm3(ps[:, B_V, :], lambda k: ctx_hi[:, b, :], lambda k: ctx_lo[:, b, :],
                                   lambda k: slot_mem(slot)[:, 512:1024], lambda k: slot_mem(slot)[:, 1536:2048], 1, v_mm)
                else:
                    yield from project(kind(g) + "v", g, B_V, v_mm)

            def beta_project(g):
                if is_attn(g) and kind(g) == "a0":
                    a = attn_index(g)
                    pe.wait_ge(beta_w_ready, 1)
                    pe.wait_ge(o_ready, a - 1)
                    yield from mm3(ps[:, B_O, 0:NH], lambda k: a_hi[:, g % 2, k, :], lambda k: a_lo[:, g % 2, k, :],
                                   lambda k: beta_w[:, 0, k, :], lambda k: beta_w[:, 1, k, :], KT, beta_mm)

            def sign_project(g):
                if not (in_run(g) and kind(g) == "f1"):
                    return
                n = g - stage_tiles("f1")[0]
                pe.wait_ge(sign_done, 1)
                pe.wait_ge(a_ready, g + 1)
                if n == 0:
                    pe.wait_ge(qk_ready, 4 * TILES)
                if n >= 2:
                    pe.wait_ge(x_new, g - 1)
                for k in range(KT):
                    for j, part in enumerate((a_hi, a_lo)):
                        last = nc.tensor.matmul(ps[:, B_Q + g % 2, :], part[:, g % 2, k, :],
                                                weight(UNITS[UNIT["sign"]][2][0], k), start=(k == 0 and j == 0),
                                                stop=(k == KT - 1 and j == 1))
                last.then_inc(sign_mm, 1)

            def blocks(dst, lhs, rhs, hs=slice(0, NH)):
                for h in range(hs.start, hs.stop):
                    for b in range(BPT):
                        rows = slice(S * b, S * (b + 1))
                        last = nc.tensor.matmul(dst(h, rows), lhs(h, rows), rhs(h, rows), start=True, stop=True)
                return last

            def col(ap):
                return lambda h, rows: ap[rows, S * h:S * (h + 1)]

            def score(g):
                a = attn_index(g)
                pe.wait_ge(qk_ready, a + 1)
                if a == 2 * TILES:
                    pe.wait_ge(x_new, 3 * TILES)
                if a:
                    pe.wait_ge(shifted, a)
                blocks(col(ps[:, B_S, :]), col(qT), col(kT)).then_inc(score_mm, 1)

            def score_kk(g):
                a = attn_index(g)
                pe.wait_ge(qk_ready, a + 1)
                if a0_index(g):
                    pe.wait_ge(u_done, 2 * a0_index(g))
                else:
                    pe.wait_ge(shifted, a)
                blocks(col(ps[:, B_S, :]), col(kT), col(kT)).then_inc(kk_mm, 1)

            def score_qk(g, half):
                pe.wait_ge(v_ready, attn_index(g) + 1)
                last = blocks(col(ps[:, B_V, :]), col(qT), col(kT), HALVES[half])
                if half:
                    last.then_inc(score_mm, 1)

            def o_transpose(g):
                if not is_attn(g):
                    return
                pe.wait_ge(o_ready, attn_index(g) + 1)
                if o_bank(g) == B_T:
                    bank_T_free()
                else:
                    pe.wait_ge(o_lo_ready, attn_index(g))
                for k in range(KT):
                    last = nc.tensor.transpose(ps[:, o_bank(g), P * k:P * (k + 1)], o_sb[:, P * k:P * (k + 1)], ident)
                last.then_inc(o_T, 1)
                issued["o_T"] += 1

            def out_project(g):
                if not is_attn(g):
                    return
                hi_slot, lo_slot = UNITS[UNIT[kind(g) + "o"]][2]
                pe.wait_ge(w_ready, UNIT[kind(g) + "o"] + 1)
                pe.wait_ge(o_lo_ready, attn_index(g) + 1)
                if g:
                    pe.wait_ge(x_new, g)
                if g == ALPHA_AT:
                    pe.wait_ge(alpha_ready, 1)
                yield from mm3(ps[:, B_Y, :], lambda k: o_hi[:, k, :], lambda k: o_lo[:, k, :],
                               lambda k: weight(hi_slot, k), lambda k: weight(lo_slot, k), KT, y_mm)

            def solve_step(g, s):
                n = a0_index(g)
                if s == 0:
                    pe.wait_ge(u0_ready, n + 1)
                    pe.wait_ge(o_lo_ready, attn_index(g) - 1)
                for half, hs in enumerate(HALVES):
                    pe.wait_ge(lk_ready, 2 * (n * (SOLVE_STEPS - 1) + s) + half + 1)
                    for h in range(hs.start, hs.stop):
                        last = nc.tensor.matmul(solve_out[:, h, :], lt_diag[:, h, :], LU[:, h, :],
                                                start=True, stop=True)
                    last.then_inc(solve_mm, 1)

            def last_solve_step(g):
                for half, hs in enumerate(HALVES):
                    pe.wait_ge(u_next, 2 * (a0_index(g) + 1) * (SOLVE_STEPS - 1) - 1 + half)
                    blocks(lambda h, r: solve_out[r, h, S:2 * S], col(LT), lambda h, r: LU[r, h, S:2 * S],
                           hs).then_inc(solve_mm, 1)

            def attend(g):
                a = attn_index(g)
                pe.wait_ge(p_ready, a + 1)
                if a:
                    pe.wait_ge(o_ready, a)
                if a == 2 * TILES:
                    pe.wait_ge(fused, MT * TILES // CHUNK)
                if kind(g) == "a0":
                    pe.wait_ge(u_done, 2 * (a0_index(g) + 1))
                    rhs = lambda h, r: LU[r, h, S:2 * S]
                else:
                    pe.wait_ge(v_ready, a + 1)
                    rhs = lambda h, r: v_sb[r, g % 2, S * h:S * (h + 1)]
                if g + 1 in A0:
                    pe.wait_ge(beta_ready, a0_index(g + 1) + 1)
                blocks(col(ps[:, B_O, :]), col(pT), rhs).then_inc(pv_mm, 1)

            def a0_slot(g):
                k, v, y = k_project(g + 1), v_project(g + 1), out_project(g - 1)
                score_kk(g)
                issue(q_project(g + 1))
                if attends_late(g - 1):
                    attend(g - 1)
                issue(k, 8)
                o_transpose(g - 1)
                issue(k, 2)
                issue(beta_project(g + 1))
                issue(k)
                solve_step(g, 0)
                score_qk(g, 0)
                issue(y, 3)
                solve_step(g, 1)
                score_qk(g, 1)
                issue(y, 3)
                solve_step(g, 2)
                issue(y)
                if transposed_here(g):
                    ln_transpose(g + 2)
                solve_step(g, 3)
                issue(v, 6)
                last_solve_step(g)
                issue(v)

            def slot(g):
                if is_attn(g):
                    score(g)
                issue(q_project(g + 1))
                if attends_late(g - 1):
                    attend(g - 1)
                o_transpose(g - 1)
                issue(k_project(g + 1))
                issue(v_project(g + 1))
                issue(beta_project(g + 1))
                if transposed_here(g):
                    ln_transpose(g + 2)
                if is_attn(g) and not attends_late(g):
                    attend(g)
                issue(out_project(g - 1))
                sign_project(g)

            pe.wait_ge(consts_loaded, 16)
            for g in RUN1:
                a0_slot(g) if g in A0 else slot(g)
            for c in range(TILES // CHUNK):
                for m in range(MT):
                    n = c * MT + m
                    bank = GU_BANKS[n % 4]
                    if n == 0:
                        pe.wait_ge(v_ready, 2 * TILES)
                        pe.wait_ge(o_ready, 2 * TILES)
                    if n >= 4:
                        pe.wait_ge(fused, n - 3)
                    if m == 0:
                        pe.wait_ge(a_ready, 2 * TILES + CHUNK * (c + 1))
                    for half, which in enumerate(("gate", "up")):
                        unit = UNIT[which + str(m // 4)]
                        pe.wait_ge(w_ready, unit + 1)
                        for k in range(KT):
                            for j, part in enumerate((a_hi, a_lo)):
                                col0 = 512 * k + P * (m % 4)
                                last = nc.tensor.matmul(
                                    ps[:, bank, CHUNK * P * half:CHUNK * P * (half + 1)],
                                    slot_mem(UNITS[unit][2][0])[:, col0:col0 + P], part[:, :, k, :],
                                    start=(k == 0 and j == 0), stop=(k == KT - 1 and j == 1))
                    last.then_inc(gu_mm, 1)
                for i in range(CHUNK):
                    ln_transpose(2 * TILES + CHUNK * (c + 1) + i)
                for i in range(CHUNK):
                    n = CHUNK * c + i
                    if c == 0:
                        pe.wait_ge(u_done, 2 * TILES)
                    else:
                        pe.wait_ge(x_new, 2 * TILES + n - 1)
                    if i == 0:
                        pe.wait_ge(fuse_ready, MT * (c + 1))
                    for m in range(MT):
                        unit = UNIT["down" + str(m // 4)]
                        pe.wait_ge(w_ready, unit + 1)
                        for j in range(2):
                            last = nc.tensor.matmul(ps[:, B_S + i, :], fuse[:, j, m, P * i:P * (i + 1)],
                                                    weight(UNITS[unit][2][0], m % 4), start=(m == 0 and j == 0),
                                                    stop=(m == MT - 1 and j == 1))
                    last.then_inc(down_mm, 1)
            for g in RUN2:
                slot(g)
                if g == ALPHA_AT:
                    pe.wait_ge(abs_done, 1)
                    pe.wait_ge(pool_consts, 2)
                    pe.wait_ge(x_new, g)
                    for k in range(KT):
                        last = nc.tensor.matmul(ps[:, B_Y, :], ones[:], raw[:, UNIT["sign"] % 2, 512 * k:512 * (k + 1)],
                                                start=(k == 0), stop=(k == KT - 1))
                    last.then_inc(alpha_mm, 1)


def kernel(**inputs):
    import concourse.bacc as bacc
    from concourse.bass_utils import run_bass_kernel_spmd

    a = {k: np.asarray(v) for k, v in inputs.items()}
    nc = bacc.Bacc("TRN2", target_bir_lowering=False, num_devices=1)
    feed = {}

    def dram(name, array):
        feed[name] = np.ascontiguousarray(array)
        return nc.dram_tensor(name, feed[name].shape, mybir.dt.from_np(feed[name].dtype), kind="ExternalInput").ap()

    def units(ap, names, rows):
        blocks = {}
        for i, name in enumerate(names):
            part = ap[512 * i:512 * (i + 1), :] if rows else ap[:, 512 * i:512 * (i + 1)]
            blocks[name] = part.rearrange("(k p) n -> p k n", p=P)
        return blocks

    w = {}
    for s in "01":
        w |= units(dram(f"x{s}_wq", a[f"L{s}_xattn_Wq"].T), [f"x{s}q"], False)
        w[f"x{s}kv"] = dram(f"x{s}_wkv", a[f"L{s}_xattn_Wkv_expand"].T)
        w |= units(dram(f"x{s}_wo", a[f"L{s}_xattn_Wout"].T), [f"x{s}o"], False)
    for c in "qkvo":
        w |= units(dram(f"a0_w{c}", a[f"L0_attn_W{c}"]), [f"a0{c}"], False)
    w |= units(dram("gate_w", a["L0_ffn_gate_w"]), ["gate0", "gate1", "gate2"], False)
    w |= units(dram("up_w", a["L0_ffn_up_w"]), ["up0", "up1", "up2"], False)
    w |= units(dram("down_w", a["L0_ffn_down_w"]), ["down0", "down1", "down2"], True)
    w |= units(dram("a1_wqkv", a["L1_attn_qkv_w"].T), ["a1q", "a1k", "a1v"], False)
    w |= units(dram("a1_wo", a["L1_attn_out_w"].T), ["a1o"], False)
    w |= units(dram("f1_w", a["L1_ffn_weight"].T), ["sign"], False)
    vec = {
        "Wb": dram("Wb", a["L0_attn_Wb"]), "bb": dram("bb", a["L0_attn_bb"]),
        "slopes": dram("slopes", a["L1_attn_alibi_slopes"]), "down_scale": dram("down_scale", a["L0_ffn_down_scale"]),
        "gate_scale": dram("gate_scale", a["L0_ffn_gate_scale"].reshape(MT, P).T),
        "up_scale": dram("up_scale", a["L0_ffn_up_scale"].reshape(MT, P).T),
        "out_b": dram("out_b", a["L1_attn_out_b"]), "qkv_b": dram("qkv_b", a["L1_attn_qkv_b"]),
        "ffn_b": dram("ffn_b", a["L1_ffn_bias"]),
    }
    x = dram("x", a["x"].reshape(NB * S, H))
    ctxT = dram("ctxT", a["ctx_512"].transpose(2, 0, 1).reshape(CTX_L, NB * CTX_S))
    consts = dram("shape_constants", shape_constants())
    out = nc.dram_tensor("out", (NB * S, H), F32, kind="ExternalOutput").ap()
    build(nc, x, ctxT, consts, w, vec, out)
    r = run_bass_kernel_spmd(nc, [feed], core_ids=[0])
    return r.results[0]["out"].reshape(NB, S, H)
```

```python
from contextlib import ExitStack

import numpy as np
import concourse.bass as bass
from concourse import mybir

F32 = mybir.dt.float32
F32R = mybir.dt.float32r
FP8 = mybir.dt.float8e4
ALU = mybir.AluOpType
ACT = mybir.ActivationFunctionType
AX_X = mybir.AxisListType.X

P = 128
NB, S, H = 32, 32, 512
NH, HD = 16, 32
CTX_L, CTX_S = 128, 257
INNER = 1536
KT = H // P
TILES = NB * S // P
BPT = P // S
STAGES = ("x0", "a0", "f0", "x1", "a1", "f1")
ATTN = ("x0", "a0", "x1", "a1")
SOLVE_STEPS = 5
CHUNK = 2
MT = INNER // P
MASKED = -1e30
SCALE = float(1.0 / np.sqrt(np.float32(HD)))
EPS = 1e-5

C_IDENT, C_CAUSAL, C_STRICT, C_COS, C_SIN, C_REL, C_NOTFIRST, C_END = np.cumsum([0, P, S, S, HD, HD, S, 1])


def shape_constants():
    half = HD // 2
    c = np.zeros((P, C_END), np.float32)
    pos = np.arange(P) % S
    keys = np.arange(S)
    c[:, C_IDENT:C_CAUSAL] = np.eye(P)
    c[:, C_CAUSAL:C_STRICT] = np.where(keys[None] <= pos[:, None], 0.0, MASKED)
    c[:, C_STRICT:C_COS] = np.where(keys[None] < pos[:, None], 0.0, MASKED)
    inv_freq = np.float32(1.0) / np.float32(10000.0) ** (np.arange(half, dtype=np.float32) / np.float32(half))
    ang = pos.astype(np.float32)[:, None] * inv_freq[None]
    c[:, C_COS:C_SIN] = np.tile(np.cos(ang), (1, 2))
    c[:, C_SIN:C_REL] = np.concatenate([-np.sin(ang), np.sin(ang)], 1)
    c[:, C_REL:C_NOTFIRST] = (keys[None] - pos[:, None]).astype(np.float32)
    c[:, C_NOTFIRST] = pos > 0
    return c


SPLIT, QUANT, SIGN = "split", "quant", "sign"
UNITS = [("x0q", SPLIT, (0, 1)), ("x0kv", SPLIT, (2,)), ("x0o", SPLIT, (3, 4)),
         ("a0q", SPLIT, (5, 6)), ("a0k", SPLIT, (7, 8)), ("a0v", SPLIT, (9, 10)), ("a0o", SPLIT, (11, 12)),
         ("gate0", QUANT, (0,)), ("gate1", QUANT, (1,)), ("gate2", QUANT, (2,)),
         ("up0", QUANT, (3,)), ("up1", QUANT, (4,)), ("down0", QUANT, (5,)), ("up2", QUANT, (13,)),
         ("down1", QUANT, (6,)), ("down2", QUANT, (7,)),
         ("x1q", SPLIT, (8, 9)), ("x1kv", SPLIT, (10,)), ("x1o", SPLIT, (11, 12)),
         ("a1q", SPLIT, (0, 1)), ("a1k", SPLIT, (2, 3)), ("a1v", SPLIT, (4, 5)), ("a1o", SPLIT, (6, 7)),
         ("sign", SIGN, (13,))]
UNIT = {name: j for j, (name, _, _) in enumerate(UNITS)}
SLOTS = 14
FUSE_SLOTS = (10, 11, 12)
SIGN_AT, ALPHA_AT = 28, 29
PREPARE_AT = {"first": ["x0q", "x0kv"], -1: ["x0o"], 1: ["a0q"], 2: ["a0k"], 3: ["a0v"], 4: ["a0o"],
              ("f0", 1): ["x1q"], ("f0", 3): ["x1kv"], 23: ["x1o"],
              24: ["a1q"], 25: ["a1k"], 26: ["a1v"], 27: ["a1o"], SIGN_AT: ["sign"]}
QUARTERS = 4
BESIDE_SOLVE = [(name, i) for name in ("gate0", "gate1", "gate2", "up0", "up1", "down0") for i in range(QUARTERS)]
BESIDE_SOLVE_FROM, BESIDE_SOLVE_PLACES = TILES, 3
BESIDE_F0 = [(name, i) for name in ("up2", "down1", "down2") for i in range(QUARTERS)]
BETA_AT = 0


def kind(g):
    return STAGES[g // TILES]


def attn_index(g):
    return sum(kind(i) in ATTN for i in range(g))


def stage_tiles(name):
    s = STAGES.index(name)
    return range(s * TILES, (s + 1) * TILES)


def build(nc, x, ctxT, consts, w, vec, out):
    with ExitStack() as es:
        def sb(name, shape, dt=F32):
            return es.enter_context(nc.sbuf_tensor(name, shape, dt))

        def sem(name):
            return es.enter_context(nc.semaphore(name))

        with nc.sbuf_tensor("lt_diag", [P, NH * P], F32) as lt_diag_mem:
            lt_diag = lt_diag_mem[:].rearrange("p (h c) -> p h c", h=NH)
        late_slot = sb("late_slot", [P, KT * 512], F32R)
        wt = sb("wt", [P, SLOTS - 1, KT * 512], F32R)
        raw = sb("raw", [P, 2, KT * 512])
        fp8 = sb("fp8", [P, 3, 512], FP8)
        xres = sb("xres", [P, TILES, H])
        cst = sb("cst", [P, int(C_END)])
        ones = sb("ones", [P, P])
        neg_half = sb("neg_half", [P, 1])
        scale_bc = sb("scale_bc", [P, H])
        bias_bc = sb("bias_bc", [P, 2, H])
        gu_scale = sb("gu_scale", [P, 2, MT])
        small_bc = sb("small_bc", [P, 2, NH])
        beta_raw = sb("beta_raw", [P, KT, NH])
        beta_w = sb("beta_w", [P, 2, KT, NH], F32R)
        stats = sb("stats", [P, 2, 6])
        mean_var = sb("mean_var", [P, 2, 2])
        norm = sb("norm", [P, 2, 3])
        xn = sb("xn", [P, 2, H])
        a_hi = sb("a_hi", [P, 2, KT, P], F32R)
        a_lo = sb("a_lo", [P, 2, KT, P], F32R)
        ctx_raw = sb("ctx_raw", [P, 2, P])
        ctx_hi = sb("ctx_hi", [P, 2, P], F32R)
        ctx_lo = sb("ctx_lo", [P, 2, P], F32R)
        q_sb = sb("q_sb", [P, H])
        k_sb = sb("k_sb", [P, H])
        rot = sb("rot", [P, H])
        qT = sb("qT", [P, H])
        kT = sb("kT", [P, H])
        v_sb = sb("v_sb", [P, 2, H])
        beta = sb("beta", [P, 2, NH])
        sc = sb("sc", [P, 2, H])
        ex = sb("ex", [P, 2, H])
        row_max = sb("row_max", [P, 2, NH])
        den = sb("den", [P, 2, NH])
        rden = sb("rden", [P, 2, NH])
        lrow = sb("lrow", [P, NH])
        pT = sb("pT", [P, H])
        o_sb = sb("o_sb", [P, H])
        o_hi = sb("o_hi", [P, KT, P], F32R)
        o_lo = sb("o_lo", [P, KT, P], F32R)
        solve = sb("solve", [P, 3 * H])
        LU = solve[:, 0:2 * H].rearrange("p (h c) -> p h c", h=NH)
        LT = solve[:, 2 * H:3 * H]

        def slot_mem(n):
            return wt[:, n, :] if n < SLOTS - 1 else late_slot[:]

        fuse = wt[:, FUSE_SLOTS[0]:FUSE_SLOTS[-1] + 1, :].rearrange(
            "p s n -> p (s n)").rearrange("p (a m t) -> p a m t", a=2, m=MT)

        ps = es.enter_context(nc.psum_tensor("ps", [P, 8, 512], F32))
        B_T, B_Q, B_K, B_V, B_S, B_KK, B_O, B_Y = range(8)
        GU_BANKS = (B_Q, B_K, B_V, B_O)

        x_loaded = [sem(f"x_loaded{i}") for i in range(3)]
        consts_loaded, bcast0_loaded = sem("consts_loaded"), sem("bcast0_loaded")
        f0_vec_loaded, a1_vec_loaded = sem("f0_vec_loaded"), sem("a1_vec_loaded")
        beta_raw_loaded = sem("beta_raw_loaded")
        raw_loaded = [sem(f"raw_loaded{i}") for i in range(2)]
        ctx_loaded = [sem(f"ctx_loaded{i}") for i in range(2)]
        pool_consts, pool_step, diag_zeroed = sem("pool_consts"), sem("pool_step"), sem("diag_zeroed")
        vec_step = sem("vec_step")
        w_hi, w_ready = sem("w_hi"), sem("w_ready")
        w_clipped, fp8_written, fp8_done = sem("w_clipped"), sem("fp8_written"), sem("fp8_done")
        sign_done, abs_done, alpha_mm, alpha_ready = sem("sign_done"), sem("abs_done"), sem("alpha_mm"), sem("alpha_ready")
        beta_hi, beta_w_ready = sem("beta_hi"), sem("beta_w_ready")
        stats_ready, rstd_ready, xn_ready = sem("stats_ready"), sem("rstd_ready"), sem("xn_ready")
        ln_T, a_hi_ready, a_ready = sem("ln_T"), sem("a_hi_ready"), sem("a_ready")
        ctx_hi_ready, ctx_ready = sem("ctx_hi_ready"), sem("ctx_ready")
        rope_terms_ready, rotated = sem("rope_terms_ready"), sem("rotated")
        q_mm, k_mm, v_mm, beta_mm = sem("q_mm"), sem("k_mm"), sem("v_mm"), sem("beta_mm")
        qk_ready, v_ready, beta_ready = sem("qk_ready"), sem("v_ready"), sem("beta_ready")
        kk_mm, score_mm = sem("kk_mm"), sem("score_mm")
        kk_shifted, shifted, kk_exp, exp_done = sem("kk_shifted"), sem("shifted"), sem("kk_exp"), sem("exp_done")
        u0_ready, lt_ready, solve_mm, u_next, lk_ready, u_done = (
            sem("u0_ready"), sem("lt_ready"), sem("solve_mm"), sem("u_next"), sem("lk_ready"), sem("u_done"))
        p_ready, pv_mm, o_ready = sem("p_ready"), sem("pv_mm"), sem("o_ready")
        o_T, o_hi_ready, o_lo_ready, y_mm = sem("o_T"), sem("o_hi_ready"), sem("o_lo_ready"), sem("y_mm")
        x_new = sem("x_new")
        gu_mm, silu_ready, fused, fuse_hi, fuse_ready, down_mm = (
            sem("gu_mm"), sem("silu_ready"), sem("fused"), sem("fuse_hi"), sem("fuse_ready"), sem("down_mm"))
        bias_added, sign_mm, stored = sem("bias_added"), sem("sign_mm"), sem("stored")

        def quarter_of(unit_mem, i):
            return unit_mem[:, 512 * i:512 * (i + 1)]

        def heads(ap):
            return ap.rearrange("p (h c) -> p h c", h=NH)

        def per_head(ap):
            return ap.unsqueeze(2).broadcast_to([P, NH, S])

        def every_head(ap):
            return ap.unsqueeze(1).broadcast_to([P, NH, S])

        ident = cst[:, C_IDENT:C_CAUSAL]
        block = es.enter_context(nc.Block())

        A0 = stage_tiles("a0")
        RUN1, RUN2 = range(-3, 2 * TILES + 1), range(3 * TILES - 1, 6 * TILES + 1)

        def in_run(g):
            return 0 <= g < 6 * TILES and kind(g) != "f0"

        def is_attn(g):
            return in_run(g) and kind(g) in ATTN

        def a0_index(g):
            return g - A0[0]

        def attends_late(g):
            return is_attn(g) and kind(g) == "a0"

        def o_bank(g):
            return B_T if is_attn(g + 1) and kind(g + 1) == "a0" else B_KK

        def ctx_index(g):
            return g if kind(g) == "x0" else TILES + g - stage_tiles("x1")[0]

        def ctx_tile(n):
            return n if n < TILES else stage_tiles("x1")[0] + n - TILES

        def normalised_here(g):
            return 0 <= g + 3 <= 2 * TILES + 2 or 3 * TILES + 2 <= g + 3 < 6 * TILES

        def transposed_here(g):
            return 0 <= g + 2 < 2 * TILES + CHUNK or 3 * TILES + CHUNK <= g + 2 < 6 * TILES

        def f0_normalised(c):
            return [g for g in range(2 * TILES + CHUNK * (c + 1), 2 * TILES + CHUNK * (c + 2)) if g > 2 * TILES + 2]

        def a_free(eng, g):
            if g < 2:
                return
            k = kind(g - 2)
            if k in ATTN:
                eng.wait_ge(v_mm, attn_index(g - 2) + 1)
                if k == "a0":
                    eng.wait_ge(beta_mm, a0_index(g - 2) + 1)
            elif k == "f0":
                eng.wait_ge(gu_mm, MT * ((g - 2 - 2 * TILES) // CHUNK + 1))
            else:
                eng.wait_ge(sign_mm, g - 2 - stage_tiles("f1")[0] + 1)

        def ln_bank(g):
            return B_Y if 2 * TILES + CHUNK <= g < 3 * TILES + CHUNK and g % 2 else B_T

        def quarter_at(g, place):
            return BESIDE_SOLVE_PLACES * (g - BESIDE_SOLVE_FROM) + place

        def slots_free(eng, name):
            stage = name[:2]
            if name[:4] == "gate":
                eng.wait_ge(v_mm, TILES)
            elif name in ("up0", "up1"):
                eng.wait_ge(y_mm, TILES)
            elif name[:4] == "down" or name == "x1q":
                eng.wait_ge(v_mm, 2 * TILES)
            elif name == "up2":
                eng.wait_ge(u_done, 2 * TILES)
            elif name in ("x1kv", "x1o"):
                eng.wait_ge(down_mm, TILES)
            elif stage == "a1" or name == "sign":
                eng.wait_ge(gu_mm, MT * TILES // CHUNK)
                eng.wait_ge(down_mm, TILES)

        HALVES = (slice(0, NH // 2), slice(NH // 2, NH))
        solve_out = ps[:, B_S:B_S + 2, :].rearrange("p b n -> p (b n)").rearrange("p (h c) -> p h c", h=NH)

        @block.sync
        def _(sp):
            xv = x.rearrange("(t p) d -> p t d", p=P)
            sp.dma_start(xres[:, 0:1, :], xv[:, 0:1, :]).then_inc(x_loaded[0], 16)
            sp.dma_start(cst[:], consts).then_inc(consts_loaded, 16)

            def load_unit(j):
                name, how, slots = UNITS[j]
                if j >= 2:
                    sp.wait_ge(w_ready, j - 1)
                dst = raw[:, j % 2, :]
                if name.endswith("kv"):
                    dst = dst[:, 0:1024]
                else:
                    dst = dst.rearrange("p (k n) -> p k n", k=KT)
                sp.dma_start(dst, w[name]).then_inc(raw_loaded[j % 2], 16)

            load_unit(0)
            sp.dma_start(xres[:, 1:3, :], xv[:, 1:3, :]).then_inc(x_loaded[1], 16)
            load_unit(1)
            sp.dma_start(xres[:, 3:TILES, :], xv[:, 3:TILES, :]).then_inc(x_loaded[2], 16)
            sp.dma_start(beta_raw[:], vec["Wb"].rearrange("(k p) n -> p k n", p=P)).then_inc(beta_raw_loaded, 16)
            sp.dma_start(small_bc[:, 0, :], vec["bb"].partition_broadcast(P)).then_inc(bcast0_loaded, 16)
            sp.dma_start(small_bc[:, 1, :], vec["slopes"].partition_broadcast(P)).then_inc(bcast0_loaded, 16)
            sp.dma_start(scale_bc[:], vec["down_scale"].partition_broadcast(P)).then_inc(f0_vec_loaded, 16)
            sp.dma_start(gu_scale[:, 0, :], vec["gate_scale"]).then_inc(f0_vec_loaded, 16)
            sp.dma_start(gu_scale[:, 1, :], vec["up_scale"]).then_inc(f0_vec_loaded, 16)
            for j in range(2, UNIT["a1q"]):
                load_unit(j)
            sp.wait_ge(pv_mm, 2 * TILES)
            sp.dma_start(solve[:], vec["qkv_b"].partition_broadcast(P)).then_inc(a1_vec_loaded, 16)
            sp.wait_ge(w_ready, UNIT["down2"] + 1)
            sp.dma_start(bias_bc[:, 0, :], vec["out_b"].partition_broadcast(P)).then_inc(a1_vec_loaded, 16)
            sp.dma_start(bias_bc[:, 1, :], vec["ffn_b"].partition_broadcast(P)).then_inc(a1_vec_loaded, 16)
            for j in range(UNIT["a1q"], len(UNITS)):
                load_unit(j)
            ov = out.rearrange("(t p) d -> p t d", p=P)
            for g in stage_tiles("f1"):
                sp.wait_ge(x_new, g + 1)
                sp.dma_start(ov[:, g % TILES, :], xres[:, g % TILES, :]).then_inc(stored, 16)
            sp.wait_ge(stored, 16 * TILES)

        @block.gpsimd
        def _(pool):
            steps = 0
            nc.gpsimd.memset(neg_half[:], -0.5).then_inc(pool_consts, 1)
            nc.gpsimd.memset(ones[:], 1.0).then_inc(pool_consts, 1)
            nc.gpsimd.memset(lt_diag[:], 0.0).then_inc(diag_zeroed, 1)
            ctx_view = ctxT.rearrange("l (b k) -> l b k", k=CTX_S)

            def load_ctx(n):
                t = n % TILES
                if n >= 2:
                    pool.wait_ge(ctx_ready, n - 1)
                pool.dma_start(ctx_raw[:, n % 2, :].rearrange("p (b k) -> p b k", b=BPT),
                               ctx_view[:, BPT * t:BPT * (t + 1), 0:S]).then_inc(ctx_loaded[n % 2], 16)

            def add_bias(g):
                if g == stage_tiles("f1")[0]:
                    pool.wait_ge(a1_vec_loaded, 48)
                pool.wait_ge(xn_ready, g + 1)
                nc.gpsimd.tensor_tensor(xres[:, g % TILES, :], xres[:, g % TILES, :], bias_bc[:, 1, :],
                                        ALU.add).then_inc(bias_added, 1)

            load_ctx(0)
            load_ctx(1)
            pool.wait_ge(pool_consts, 2)
            for g in range(6 * TILES):
                b = g % 2
                pool.wait_ge(stats_ready, g + 1)
                if g >= 2:
                    pool.wait_ge(xn_ready, g - 1)
                nc.gpsimd.tensor_scalar(norm[:, b, 0:1], mean_var[:, b, 1:2], EPS, None, ALU.add).then_inc(pool_step, 1)
                steps += 1
                pool.wait_ge(pool_step, steps)
                nc.gpsimd.tensor_tensor(norm[:, b, 1:2], norm[:, b, 0:1], neg_half[:], ALU.pow).then_inc(pool_step, 1)
                steps += 1
                pool.wait_ge(pool_step, steps)
                nc.gpsimd.tensor_scalar(norm[:, b, 2:3], mean_var[:, b, 0:1], -1.0, norm[:, b, 1:2],
                                        ALU.mult, ALU.mult).then_inc(rstd_ready, 1)
                if g - 1 in stage_tiles("f1"):
                    add_bias(g - 1)
                if g - 2 in A0:
                    for which, dst in enumerate((q_sb, k_sb)):
                        pool.wait_ge(rope_terms_ready, 2 * a0_index(g - 2) + which + 1)
                        nc.gpsimd.tensor_tensor(dst[:], dst[:], rot[:], ALU.add).then_inc(rotated, 1)
                for n in range(2, 2 * TILES):
                    if g == (n + 2 if n in (TILES, TILES + 1) else ctx_tile(n)):
                        load_ctx(n)
            add_bias(6 * TILES - 1)

        @block.scalar
        def _(act):
            split_jobs = [0]
            quarters = [0]
            ctx_tiles = [0]

            def quant_quarter(name, i):
                x = quarter_of(raw[:, UNIT[name] % 2, :], i)
                q = quarters[0]
                quarters[0] += 1
                act.wait_ge(w_clipped, q + 1)
                if q:
                    act.wait_ge(fp8_done, q)
                nc.scalar.activation(fp8[:, 2, :], x, ACT.Copy, scale=0.25, saturate=False).then_inc(fp8_written, 1)
                act.wait_ge(fp8_written, q + 1)
                nc.scalar.activation(x, fp8[:, 2, :], ACT.Copy, scale=4.0).then_inc(fp8_done, 1)

            def prepare(name):
                j = UNIT[name]
                _, how, slots = UNITS[j]
                if how != QUANT:
                    act.wait_ge(raw_loaded[j % 2], 16 * (j // 2 + 1))
                slots_free(act, name)
                r = raw[:, j % 2, :]
                if how == SPLIT:
                    if name.endswith("kv"):
                        dst, r = slot_mem(slots[0])[:, 0:1024], r[:, 0:1024]
                    else:
                        dst = slot_mem(slots[0])
                    nc.scalar.activation(dst, r, ACT.Copy).then_inc(w_hi, 1)
                else:
                    act.wait_ge(sign_done, 1)
                    nc.scalar.activation(r, r, ACT.Abs).then_inc(abs_done, 1)

            def normalise(g):
                act.wait_ge(rstd_ready, g + 1)
                if g >= 2:
                    act.wait_ge(ln_T, g - 1)
                nc.scalar.activation(xn[:, g % 2, :], xres[:, g % TILES, :], ACT.Identity,
                                     scale=norm[:, g % 2, 1:2], bias=norm[:, g % 2, 2:3]).then_inc(xn_ready, 1)

            def split_a(g):
                act.wait_ge(ln_T, g + 1)
                a_free(act, g)
                nc.scalar.activation(a_hi[:, g % 2, :, :], ps[:, ln_bank(g), :].rearrange("p (k t) -> p k t", k=KT),
                                     ACT.Copy).then_inc(a_hi_ready, 1)

            def split_ctx(g):
                n = ctx_tiles[0]
                ctx_tiles[0] += 1
                act.wait_ge(ctx_loaded[n % 2], 16 * (n // 2 + 1))
                if n >= 2:
                    act.wait_ge(v_mm, attn_index(ctx_tile(n - 2)) + 1)
                nc.scalar.activation(ctx_hi[:, n % 2, :], ctx_raw[:, n % 2, :], ACT.Copy).then_inc(ctx_hi_ready, 1)

            def exponentials(g):
                act.wait_ge(shifted, attn_index(g) + 1)
                nc.scalar.activation(ex[:, 0, :], sc[:, 0, :], ACT.Exp).then_inc(exp_done, 1)

            def split_o(g):
                if is_attn(g):
                    a = attn_index(g)
                    act.wait_ge(o_T, a + 1)
                    if a:
                        act.wait_ge(y_mm, a)
                    nc.scalar.activation(o_hi[:], ps[:, o_bank(g), :].rearrange("p (k t) -> p k t", k=KT),
                                         ACT.Copy).then_inc(o_hi_ready, 1)

            def take_v(g):
                if not is_attn(g) or kind(g) == "a1":
                    return
                a = attn_index(g)
                act.wait_ge(v_mm, a + 1)
                if a >= 2:
                    act.wait_ge(pv_mm, a - 1)
                if a >= TILES + 2:
                    act.wait_ge(u0_ready, min(a - 1 - TILES, TILES))
                nc.scalar.activation(v_sb[:, g % 2, :], ps[:, B_V, :], ACT.Copy).then_inc(v_ready, 1)

            def take_a(g):
                if transposed_here(g - 2):
                    if kind(g)[0] == "x":
                        split_ctx(g)
                    split_a(g)

            def spread_lt(hs):
                for b in range(BPT):
                    rows = slice(S * b, S * (b + 1))
                    last = nc.scalar.activation(lt_diag[rows, hs, rows], heads(LT)[rows, hs, :], ACT.Copy)
                last.then_inc(lk_ready, 1)

            def next_lk(g, s):
                for half, hs in enumerate(HALVES):
                    act.wait_ge(u_next, 2 * (a0_index(g) * (SOLVE_STEPS - 1) + s) + half + 1)
                    nc.scalar.activation(LU[:, hs, 0:S], solve_out[:, hs, 0:S], ACT.Copy)
                    spread_lt(hs)

            def a0_slot(g):
                a = attn_index(g)
                quant_quarter(*BESIDE_SOLVE[quarter_at(g, 0)])
                act.wait_ge(kk_shifted, a0_index(g) + 1)
                nc.scalar.activation(ex[:, 1, :], sc[:, 1, :], ACT.Exp).then_inc(kk_exp, 1)
                act.wait_ge(v_ready, a + 1)
                act.wait_ge(pv_mm, a)
                nc.scalar.activation(LU[:, :, S:2 * S], heads(v_sb[:, g % 2, :]), ACT.Copy).then_inc(u0_ready, 1)
                for half, hs in enumerate(HALVES):
                    act.wait_ge(lt_ready, 2 * a0_index(g) + half + 1)
                    act.wait_ge(diag_zeroed, 1)
                    spread_lt(hs)
                if normalised_here(g):
                    normalise(g + 3)
                next_lk(g, 0)
                split_o(g - 1)
                next_lk(g, 1)
                quant_quarter(*BESIDE_SOLVE[quarter_at(g, 1)])
                next_lk(g, 2)
                quant_quarter(*BESIDE_SOLVE[quarter_at(g, 2)])
                take_a(g + 2)
                exponentials(g)
                take_v(g + 1)

            def slot(g):
                if g != SIGN_AT:
                    for name in PREPARE_AT.get(g, ()):
                        prepare(name)
                if is_attn(g):
                    exponentials(g)
                split_o(g - 1)
                if is_attn(g) and normalised_here(g):
                    normalise(g + 3)
                take_v(g + 1)
                take_a(g + 2)
                if not is_attn(g) and normalised_here(g):
                    normalise(g + 3)
                if g == SIGN_AT:
                    prepare("sign")

            for g in RUN1:
                a0_slot(g) if g in A0 else slot(g)
                if g == RUN1[0]:
                    for name in PREPARE_AT["first"]:
                        prepare(name)
                if g == BETA_AT:
                    act.wait_ge(beta_raw_loaded, 16)
                    nc.scalar.activation(beta_w[:, 0], beta_raw[:], ACT.Copy).then_inc(beta_hi, 1)
            act.wait_ge(f0_vec_loaded, 48)
            for c in range(TILES // CHUNK):
                for m in range(MT + 1):
                    n = c * MT + m
                    if m == 3:
                        for g in f0_normalised(c):
                            normalise(g)
                    if m < MT:
                        act.wait_ge(gu_mm, n + 1)
                        if n >= 2:
                            act.wait_ge(fused, n - 1)
                        nc.scalar.activation(ex[:, m % 2, 0:CHUNK * P], ps[:, GU_BANKS[n % 4], 0:CHUNK * P], ACT.Silu,
                                             scale=gu_scale[:, 0, m:m + 1]).then_inc(silu_ready, 1)
                    if m:
                        act.wait_ge(fused, n)
                        if m == 1:
                            act.wait_ge(y_mm, 2 * TILES)
                            if c:
                                act.wait_ge(down_mm, CHUNK * c)
                        nc.scalar.activation(fuse[:, 0, m - 1, :], sc[:, (m - 1) % 2, 0:CHUNK * P],
                                             ACT.Copy).then_inc(fuse_hi, 1)
                    if c == 0 and m:
                        quant_quarter(*BESIDE_F0[m - 1])
                for i in range(CHUNK):
                    g = 2 * TILES + CHUNK * (c + 1) + i
                    if kind(g)[0] == "x":
                        split_ctx(g)
                    split_a(g)
                for name in PREPARE_AT.get(("f0", c), ()):
                    prepare(name)
            for g in RUN2:
                slot(g)

        @block.vector
        def _(dve):
            steps = [0]
            splits = [0]
            ctx_tiles = [0]

            def step(ins):
                ins.then_inc(vec_step, 1)
                steps[0] += 1
                dve.wait_ge(vec_step, steps[0])

            def clip_quarter(q, name, i):
                j = UNIT[name]
                if i == 0:
                    dve.wait_ge(raw_loaded[j % 2], 16 * (j // 2 + 1))
                nc.vector.tensor_scalar(fp8[:, q % 2, :], quarter_of(raw[:, j % 2, :], i), 240.0, -240.0,
                                        ALU.min, ALU.max, saturate=False).then_inc(w_clipped, 1)

            def add_quarter(q, name, i):
                j = UNIT[name]
                x, part = quarter_of(raw[:, j % 2, :], i), bias_bc[:, 0, :]
                dve.wait_ge(fp8_done, q + 1)
                step(nc.vector.scalar_tensor_tensor(out=part, in0=x, scalar=240.0, in1=fp8[:, q % 2, :],
                                                    op0=ALU.max, op1=ALU.add))
                if i == 0:
                    slots_free(dve, name)
                last = nc.vector.scalar_tensor_tensor(out=quarter_of(slot_mem(UNITS[j][2][0]), i), in0=x,
                                                      scalar=-240.0, in1=part, op0=ALU.min, op1=ALU.add)
                if i == QUARTERS - 1:
                    last.then_inc(w_ready, 1)
                    dve.wait_ge(w_ready, j + 1)
                else:
                    step(last)

            def quarter_beside_solve(g, place):
                q = quarter_at(g, place)
                add_quarter(q, *BESIDE_SOLVE[q])
                if q + 1 < len(BESIDE_SOLVE):
                    clip_quarter(q + 1, *BESIDE_SOLVE[q + 1])

            def prepare(name):
                j = UNIT[name]
                _, how, slots = UNITS[j]
                r = raw[:, j % 2, :]
                if how == SPLIT:
                    splits[0] += 1
                    dve.wait_ge(w_hi, splits[0])
                    if name.endswith("kv"):
                        hi, lo, r = slot_mem(slots[0])[:, 0:1024], slot_mem(slots[0])[:, 1024:2048], r[:, 0:1024]
                    else:
                        hi, lo = slot_mem(slots[0]), slot_mem(slots[1])
                    nc.vector.tensor_tensor(lo, r, hi.bitcast(F32), ALU.subtract).then_inc(w_ready, 1)
                elif how == SIGN:
                    dve.wait_ge(raw_loaded[j % 2], 16 * (j // 2 + 1))
                    slots_free(dve, name)
                    dst = slot_mem(slots[0])
                    step(nc.vector.tensor_scalar(dst, r, 0.0, 2.0, ALU.is_ge, ALU.mult))
                    nc.vector.tensor_scalar(dst, dst.bitcast(F32), -1.0, None, ALU.add).then_inc(sign_done, 1)

            def ln_stats(g):
                if g < TILES:
                    dve.wait_ge(x_loaded[0 if g == 0 else 1 if g < 3 else 2], 16)
                else:
                    dve.wait_ge(x_new, g - TILES + 1)
                if g >= 2:
                    dve.wait_ge(rstd_ready, g - 1)
                step(nc.vector.bn_stats(stats[:, g % 2, :], xres[:, g % TILES, :]))
                nc.vector.bn_aggr(mean_var[:, g % 2, :], stats[:, g % 2, :]).then_inc(stats_ready, 1)

            def split_a(g):
                dve.wait_ge(a_hi_ready, g + 1)
                nc.vector.tensor_tensor(a_lo[:, g % 2, :, :], ps[:, ln_bank(g), :].rearrange("p (k t) -> p k t", k=KT),
                                        a_hi[:, g % 2, :, :].bitcast(F32), ALU.subtract).then_inc(a_ready, 1)

            def split_ctx(g):
                n = ctx_tiles[0]
                ctx_tiles[0] += 1
                dve.wait_ge(ctx_hi_ready, n + 1)
                nc.vector.tensor_tensor(ctx_lo[:, n % 2, :], ctx_raw[:, n % 2, :], ctx_hi[:, n % 2, :].bitcast(F32),
                                        ALU.subtract).then_inc(ctx_ready, 1)

            def softmax_shift(bank, buf, mask, done):
                in1 = heads(rot[:]) if mask is None else every_head(mask)
                step(nc.vector.scalar_tensor_tensor(out=heads(sc[:, buf, :]), in0=heads(ps[:, bank, :]), scalar=SCALE,
                                                    in1=in1, op0=ALU.mult, op1=ALU.add))
                step(nc.vector.tensor_reduce(row_max[:, buf, :], heads(sc[:, buf, :]), AX_X, ALU.max))
                nc.vector.tensor_tensor(heads(sc[:, buf, :]), heads(sc[:, buf, :]), per_head(row_max[:, buf, :]),
                                        ALU.subtract).then_inc(done, 1)

            def rope_terms(bank, dst):
                src = ps[:, bank, :].rearrange("p (h a c) -> p h a c", h=NH, a=2)
                halves = rot[:].rearrange("p (h a c) -> p h a c", h=NH, a=2)
                half = HD // 2
                nc.vector.tensor_tensor(heads(dst), heads(ps[:, bank, :]), every_head(cst[:, C_COS:C_SIN]), ALU.mult)
                for a in range(2):
                    sin = cst[:, C_SIN + half * a:C_SIN + half * (a + 1)]
                    last = nc.vector.tensor_tensor(halves[:, :, a, :], src[:, :, 1 - a, :],
                                                   sin.unsqueeze(1).broadcast_to([P, NH, half]), ALU.mult)
                last.then_inc(rope_terms_ready, 1)

            def rotate_q(g):
                if is_attn(g) and kind(g) == "a0":
                    dve.wait_ge(q_mm, attn_index(g) + 1)
                    if a0_index(g):
                        dve.wait_ge(rotated, 2 * a0_index(g))
                    rope_terms(B_Q, q_sb[:])

            def take_q(g):
                if not is_attn(g):
                    return
                a = attn_index(g)
                dve.wait_ge(q_mm, a + 1)
                if kind(g) == "a1":
                    step(nc.vector.tensor_tensor(q_sb[:], ps[:, B_Q, :], solve[:, 0:H], ALU.add))
                if kind(g) == "a0":
                    dve.wait_ge(rotated, 2 * a0_index(g) + 1)
                if a:
                    dve.wait_ge(score_mm, a)
                step(nc.vector.transpose(qT[:], ps[:, B_Q, :] if kind(g)[0] == "x" else q_sb[:]))

            def rotate_k(g):
                if is_attn(g) and kind(g) == "a0":
                    dve.wait_ge(k_mm, attn_index(g) + 1)
                    dve.wait_ge(rotated, 2 * a0_index(g) + 1)
                    rope_terms(B_K, k_sb[:])

            def take_k(g):
                if not is_attn(g):
                    return
                dve.wait_ge(k_mm, attn_index(g) + 1)
                if kind(g) == "a1":
                    step(nc.vector.tensor_tensor(k_sb[:], ps[:, B_K, :], solve[:, H:2 * H], ALU.add))
                if kind(g) == "a0":
                    dve.wait_ge(rotated, 2 * a0_index(g) + 2)
                nc.vector.transpose(kT[:], ps[:, B_K, :] if kind(g)[0] == "x" else k_sb[:]).then_inc(qk_ready, 1)

            def take_rest(g):
                if not in_run(g):
                    return
                if kind(g) == "a0":
                    n = a0_index(g)
                    dve.wait_ge(bcast0_loaded, 32)
                    dve.wait_ge(beta_mm, n + 1)
                    nc.vector.tensor_tensor(beta[:, g % 2, :], ps[:, B_O, 0:NH], small_bc[:, 0, :],
                                            ALU.add).then_inc(beta_ready, 1)
                elif kind(g) == "a1":
                    a = attn_index(g)
                    dve.wait_ge(v_mm, a + 1)
                    dve.wait_ge(pv_mm, a - 1)
                    nc.vector.tensor_tensor(v_sb[:, g % 2, :], ps[:, B_V, :], solve[:, 2 * H:3 * H],
                                            ALU.add).then_inc(v_ready, 1)

            def take_sign(g):
                if in_run(g) and kind(g) == "f1":
                    n = g - stage_tiles("f1")[0]
                    if n == 0:
                        dve.wait_ge(alpha_ready, 1)
                    dve.wait_ge(sign_mm, n + 1)
                    step(nc.vector.tensor_tensor(k_sb[:], ps[:, B_Q + g % 2, :], scale_bc[:], ALU.mult))
                    dve.wait_ge(bias_added, n + 1)
                    nc.vector.tensor_tensor(xres[:, g % TILES, :], xres[:, g % TILES, :], k_sb[:],
                                            ALU.add).then_inc(x_new, 1)
                    dve.wait_ge(x_new, g + 1)

            def residual(g):
                if not is_attn(g):
                    return
                t = g % TILES
                dve.wait_ge(y_mm, attn_index(g) + 1)
                if kind(g) == "a1":
                    step(nc.vector.tensor_tensor(xres[:, t, :], xres[:, t, :], bias_bc[:, 0, :], ALU.add))
                nc.vector.tensor_tensor(xres[:, t, :], xres[:, t, :], ps[:, B_Y, :], ALU.add).then_inc(x_new, 1)

            def take_a(g):
                if transposed_here(g - 2):
                    if kind(g)[0] == "x":
                        split_ctx(g)
                    split_a(g)

            def stats_next(g):
                if normalised_here(g):
                    ln_stats(g + 3)

            def o_norm(g):
                if is_attn(g):
                    a = attn_index(g)
                    dve.wait_ge(pv_mm, a + 1)
                    if a:
                        dve.wait_ge(o_T, a)
                    nc.vector.tensor_tensor(heads(o_sb[:]), heads(ps[:, B_O, :]), per_head(rden[:, 0, :]),
                                            ALU.mult).then_inc(o_ready, 1)

            def split_o(g):
                if is_attn(g):
                    dve.wait_ge(o_hi_ready, attn_index(g) + 1)
                    nc.vector.tensor_tensor(o_lo[:], ps[:, o_bank(g), :].rearrange("p (k t) -> p k t", k=KT),
                                            o_hi[:].bitcast(F32), ALU.subtract).then_inc(o_lo_ready, 1)

            def causal_shift(g):
                dve.wait_ge(score_mm, attn_index(g) + 1)
                softmax_shift(B_V if kind(g) == "a0" else B_S, 0, cst[:, C_CAUSAL:C_STRICT], shifted)

            def alibi_shift(g):
                if g == stage_tiles("a1")[0]:
                    for h in range(NH):
                        last = nc.vector.scalar_tensor_tensor(
                            out=rot[:, S * h:S * (h + 1)], in0=cst[:, C_REL:C_NOTFIRST], scalar=small_bc[:, 1, h:h + 1],
                            in1=cst[:, C_CAUSAL:C_STRICT], op0=ALU.mult, op1=ALU.add)
                    step(last)
                dve.wait_ge(score_mm, attn_index(g) + 1)
                softmax_shift(B_S, 0, None, shifted)

            def transpose_p(g):
                a = attn_index(g)
                dve.wait_ge(exp_done, a + 1)
                if a:
                    dve.wait_ge(pv_mm, a)
                nc.vector.transpose(pT[:], ex[:, 0, :]).then_inc(p_ready, 1)

            def sum_p():
                step(nc.vector.tensor_reduce(den[:, 0, :], heads(ex[:, 0, :]), AX_X, ALU.add))
                step(nc.vector.reciprocal(rden[:, 0, :], den[:, 0, :]))

            def make_l(g):
                n = a0_index(g)
                dve.wait_ge(kk_mm, n + 1)
                softmax_shift(B_S, 1, cst[:, C_STRICT:C_COS], kk_shifted)
                if a0_index(g):
                    residual(g - 2)
                dve.wait_ge(kk_exp, n + 1)
                step(nc.vector.tensor_reduce(den[:, 1, :], heads(ex[:, 1, :]), AX_X, ALU.add))
                step(nc.vector.reciprocal(rden[:, 1, :], den[:, 1, :]))
                dve.wait_ge(beta_ready, n + 1)
                step(nc.vector.scalar_tensor_tensor(out=lrow[:], in0=rden[:, 1, :], scalar=cst[:, C_NOTFIRST:C_END],
                                                    in1=beta[:, g % 2, :], op0=ALU.mult, op1=ALU.mult))
                step(nc.vector.tensor_tensor(LU[:, :, 0:S], heads(ex[:, 1, :]), per_head(lrow[:]), ALU.mult))
                for hs in HALVES:
                    nc.vector.transpose(heads(LT)[:, hs, :], LU[:, hs, 0:S]).then_inc(lt_ready, 1)

            def solve_step(g, s):
                last = s == SOLVE_STEPS - 1
                for half, hs in enumerate(HALVES):
                    dve.wait_ge(solve_mm, 2 * (a0_index(g) * SOLVE_STEPS + s) + half + 1)
                    if not last:
                        nc.vector.transpose(heads(LT)[:, hs, :], solve_out[:, hs, 0:S])
                    nc.vector.tensor_tensor(LU[:, hs, S:2 * S], LU[:, hs, S:2 * S], solve_out[:, hs, S:2 * S],
                                            ALU.subtract if s == 0 else ALU.add).then_inc(u_done if last else u_next, 1)

            def a0_slot(g):
                if g == BESIDE_SOLVE_FROM:
                    clip_quarter(0, *BESIDE_SOLVE[0])
                make_l(g)
                if attends_late(g - 1):
                    sum_p()
                o_norm(g - 1)
                stats_next(g)
                solve_step(g, 0)
                rotate_q(g + 1)
                split_o(g - 1)
                solve_step(g, 1)
                take_rest(g + 1)
                quarter_beside_solve(g, 0)
                solve_step(g, 2)
                rotate_k(g + 1)
                quarter_beside_solve(g, 1)
                solve_step(g, 3)
                causal_shift(g)
                solve_step(g, 4)
                transpose_p(g)
                take_q(g + 1)
                take_k(g + 1)
                take_a(g + 2)
                quarter_beside_solve(g, 2)

            def slot(g):
                if attends_late(g - 1):
                    residual(g - 2)
                    sum_p()
                o_norm(g - 1)
                if is_attn(g):
                    alibi_shift(g) if kind(g) == "a1" else causal_shift(g)
                stats_next(g)
                if is_attn(g):
                    transpose_p(g)
                split_o(g - 1)
                if is_attn(g):
                    sum_p()
                for name in PREPARE_AT.get(g, ()):
                    prepare(name)
                rotate_q(g + 1)
                take_q(g + 1)
                if g + 1 in A0:
                    take_rest(g + 1)
                rotate_k(g + 1)
                take_k(g + 1)
                if g + 1 not in A0:
                    take_rest(g + 1)
                take_a(g + 2)
                if g != 2 * TILES:
                    residual(g - 1)
                take_sign(g)

            for g in RUN1:
                a0_slot(g) if g in A0 else slot(g)
                if g == RUN1[0]:
                    for name in PREPARE_AT["first"]:
                        prepare(name)
                    dve.wait_ge(consts_loaded, 16)
                if g == BETA_AT:
                    dve.wait_ge(beta_hi, 1)
                    nc.vector.tensor_tensor(beta_w[:, 1], beta_raw[:], beta_w[:, 0].bitcast(F32),
                                            ALU.subtract).then_inc(beta_w_ready, 1)
            dve.wait_ge(f0_vec_loaded, 48)
            for c in range(TILES // CHUNK):
                for m in range(MT + 1):
                    n = c * MT + m
                    if m == 2:
                        if c == 0:
                            residual(2 * TILES - 1)
                        for g in f0_normalised(c):
                            ln_stats(g)
                    if m < MT:
                        dve.wait_ge(silu_ready, n + 1)
                        if n >= 2:
                            dve.wait_ge(fuse_hi, n - 1)
                            dve.wait_ge(fuse_ready, n - 1)
                        nc.vector.scalar_tensor_tensor(
                            out=sc[:, m % 2, 0:CHUNK * P], in0=ps[:, GU_BANKS[n % 4], CHUNK * P:2 * CHUNK * P],
                            scalar=gu_scale[:, 1, m:m + 1], in1=ex[:, m % 2, 0:CHUNK * P], op0=ALU.mult,
                            op1=ALU.mult).then_inc(fused, 1)
                    if m:
                        dve.wait_ge(fuse_hi, n)
                        nc.vector.tensor_tensor(fuse[:, 1, m - 1, :], sc[:, (m - 1) % 2, 0:CHUNK * P],
                                                fuse[:, 0, m - 1, :].bitcast(F32), ALU.subtract).then_inc(fuse_ready, 1)
                    if c == 0:
                        if m >= 2:
                            add_quarter(len(BESIDE_SOLVE) + m - 2, *BESIDE_F0[m - 2])
                        if m < MT:
                            clip_quarter(len(BESIDE_SOLVE) + m, *BESIDE_F0[m])
                if c == 0:
                    add_quarter(len(BESIDE_SOLVE) + MT - 1, *BESIDE_F0[MT - 1])
                for i in range(CHUNK):
                    g = 2 * TILES + CHUNK * (c + 1) + i
                    if kind(g)[0] == "x":
                        split_ctx(g)
                    split_a(g)
                for i in range(CHUNK):
                    g = 2 * TILES + CHUNK * c + i
                    dve.wait_ge(down_mm, CHUNK * c + i + 1)
                    step(nc.vector.tensor_tensor(k_sb[:], ps[:, B_S + i, :], scale_bc[:], ALU.mult))
                    nc.vector.tensor_tensor(xres[:, g % TILES, :], xres[:, g % TILES, :], k_sb[:],
                                            ALU.add).then_inc(x_new, 1)
                    dve.wait_ge(x_new, g + 1)
                for name in PREPARE_AT.get(("f0", c), ()):
                    prepare(name)
            dve.wait_ge(a1_vec_loaded, 48)
            for g in RUN2:
                slot(g)
                if g == ALPHA_AT:
                    dve.wait_ge(alpha_mm, 1)
                    nc.vector.tensor_scalar(scale_bc[:], ps[:, B_Y, :], 1.0 / H, None, ALU.mult).then_inc(alpha_ready, 1)

        @block.tensor
        def _(pe):
            issued = {"ln_T": 0, "o_T in bank T": 0}

            def mm3(dst, hi, lo, w_hi_of, w_lo_of, nk, done):
                for k in range(nk):
                    nc.tensor.matmul(dst, hi(k), w_hi_of(k), start=(k == 0), stop=False)
                    yield
                    nc.tensor.matmul(dst, hi(k), w_lo_of(k), start=False, stop=False)
                    yield
                    last = nc.tensor.matmul(dst, lo(k), w_hi_of(k), start=False, stop=(k == nk - 1))
                    if k == nk - 1:
                        last.then_inc(done, 1)
                    yield

            def issue(products, n=None):
                for i, _ in enumerate(products):
                    if i + 1 == n:
                        break

            def weight(slot, k):
                return slot_mem(slot)[:, 512 * k:512 * (k + 1)]

            def bank_T_free():
                if issued["ln_T"]:
                    pe.wait_ge(a_ready, issued["ln_T"])
                if issued["o_T in bank T"]:
                    pe.wait_ge(o_lo_ready, issued["o_T in bank T"])

            def ln_transpose(g):
                pe.wait_ge(xn_ready, g + 1)
                if ln_bank(g) == B_T:
                    bank_T_free()
                elif g == 2 * TILES + CHUNK + 1:
                    pe.wait_ge(x_new, 2 * TILES)
                else:
                    pe.wait_ge(a_ready, g - 1)
                for k in range(KT):
                    last = nc.tensor.transpose(ps[:, ln_bank(g), P * k:P * (k + 1)], xn[:, g % 2, P * k:P * (k + 1)], ident)
                last.then_inc(ln_T, 1)
                issued["ln_T"] += 1

            def project(name, g, bank, done):
                hi_slot, lo_slot = UNITS[UNIT[name]][2]
                pe.wait_ge(w_ready, UNIT[name] + 1)
                pe.wait_ge(a_ready, g + 1)
                yield from mm3(ps[:, bank, :], lambda k: a_hi[:, g % 2, k, :], lambda k: a_lo[:, g % 2, k, :],
                               lambda k: weight(hi_slot, k), lambda k: weight(lo_slot, k), KT, done)

            def q_project(g):
                if not is_attn(g):
                    return
                a = attn_index(g)
                if a:
                    pe.wait_ge(qk_ready, a)
                if a == 2 * TILES:
                    pe.wait_ge(fused, MT * TILES // CHUNK)
                yield from project(kind(g) + "q", g, B_Q, q_mm)

            def k_project(g):
                if not is_attn(g):
                    return
                if kind(g)[0] == "x":
                    n = ctx_index(g)
                    pe.wait_ge(ctx_ready, n + 1)
                    pe.wait_ge(w_ready, UNIT[kind(g) + "kv"] + 1)
                    slot, b = UNITS[UNIT[kind(g) + "kv"]][2][0], n % 2
                    yield from mm3(ps[:, B_K, :], lambda k: ctx_hi[:, b, :], lambda k: ctx_lo[:, b, :],
                                   lambda k: slot_mem(slot)[:, 0:512], lambda k: slot_mem(slot)[:, 1024:1536], 1, k_mm)
                else:
                    yield from project(kind(g) + "k", g, B_K, k_mm)

            def v_project(g):
                if not is_attn(g):
                    return
                a = attn_index(g)
                if a:
                    pe.wait_ge(v_ready, a)
                if is_attn(g - 1) and kind(g - 1) == "a0":
                    pe.wait_ge(shifted, a)
                if kind(g)[0] == "x":
                    b = ctx_index(g) % 2
                    slot = UNITS[UNIT[kind(g) + "kv"]][2][0]
                    yield from mm3(ps[:, B_V, :], lambda k: ctx_hi[:, b, :], lambda k: ctx_lo[:, b, :],
                                   lambda k: slot_mem(slot)[:, 512:1024], lambda k: slot_mem(slot)[:, 1536:2048], 1, v_mm)
                else:
                    yield from project(kind(g) + "v", g, B_V, v_mm)

            def beta_project(g):
                if is_attn(g) and kind(g) == "a0":
                    a = attn_index(g)
                    pe.wait_ge(beta_w_ready, 1)
                    pe.wait_ge(o_ready, a - 1)
                    yield from mm3(ps[:, B_O, 0:NH], lambda k: a_hi[:, g % 2, k, :], lambda k: a_lo[:, g % 2, k, :],
                                   lambda k: beta_w[:, 0, k, :], lambda k: beta_w[:, 1, k, :], KT, beta_mm)

            def sign_project(g):
                if not (in_run(g) and kind(g) == "f1"):
                    return
                n = g - stage_tiles("f1")[0]
                pe.wait_ge(sign_done, 1)
                pe.wait_ge(a_ready, g + 1)
                if n == 0:
                    pe.wait_ge(qk_ready, 4 * TILES)
                if n >= 2:
                    pe.wait_ge(x_new, g - 1)
                for k in range(KT):
                    for j, part in enumerate((a_hi, a_lo)):
                        last = nc.tensor.matmul(ps[:, B_Q + g % 2, :], part[:, g % 2, k, :],
                                                weight(UNITS[UNIT["sign"]][2][0], k), start=(k == 0 and j == 0),
                                                stop=(k == KT - 1 and j == 1))
                last.then_inc(sign_mm, 1)

            def blocks(dst, lhs, rhs, hs=slice(0, NH)):
                for h in range(hs.start, hs.stop):
                    for b in range(BPT):
                        rows = slice(S * b, S * (b + 1))
                        last = nc.tensor.matmul(dst(h, rows), lhs(h, rows), rhs(h, rows), start=True, stop=True)
                return last

            def col(ap):
                return lambda h, rows: ap[rows, S * h:S * (h + 1)]

            def score(g):
                a = attn_index(g)
                pe.wait_ge(qk_ready, a + 1)
                if a == 2 * TILES:
                    pe.wait_ge(x_new, 3 * TILES)
                if a:
                    pe.wait_ge(shifted, a)
                blocks(col(ps[:, B_S, :]), col(qT), col(kT)).then_inc(score_mm, 1)

            def score_kk(g):
                a = attn_index(g)
                pe.wait_ge(qk_ready, a + 1)
                if a0_index(g):
                    pe.wait_ge(u_done, 2 * a0_index(g))
                else:
                    pe.wait_ge(shifted, a)
                blocks(col(ps[:, B_S, :]), col(kT), col(kT)).then_inc(kk_mm, 1)

            def score_qk(g, half):
                pe.wait_ge(v_ready, attn_index(g) + 1)
                last = blocks(col(ps[:, B_V, :]), col(qT), col(kT), HALVES[half])
                if half:
                    last.then_inc(score_mm, 1)

            def o_transpose(g):
                if not is_attn(g):
                    return
                pe.wait_ge(o_ready, attn_index(g) + 1)
                if o_bank(g) == B_T:
                    bank_T_free()
                else:
                    pe.wait_ge(o_lo_ready, attn_index(g))
                for k in range(KT):
                    last = nc.tensor.transpose(ps[:, o_bank(g), P * k:P * (k + 1)], o_sb[:, P * k:P * (k + 1)], ident)
                last.then_inc(o_T, 1)
                if o_bank(g) == B_T:
                    issued["o_T in bank T"] = attn_index(g) + 1

            def out_project(g):
                if not is_attn(g):
                    return
                hi_slot, lo_slot = UNITS[UNIT[kind(g) + "o"]][2]
                pe.wait_ge(w_ready, UNIT[kind(g) + "o"] + 1)
                pe.wait_ge(o_lo_ready, attn_index(g) + 1)
                if g:
                    pe.wait_ge(x_new, g)
                if g == 3 * TILES:
                    pe.wait_ge(a_ready, g + 2)
                if g == ALPHA_AT:
                    pe.wait_ge(alpha_ready, 1)
                yield from mm3(ps[:, B_Y, :], lambda k: o_hi[:, k, :], lambda k: o_lo[:, k, :],
                               lambda k: weight(hi_slot, k), lambda k: weight(lo_slot, k), KT, y_mm)

            def solve_step(g, s):
                n = a0_index(g)
                if s == 0:
                    pe.wait_ge(u0_ready, n + 1)
                    pe.wait_ge(o_lo_ready, attn_index(g) - 1)
                for half, hs in enumerate(HALVES):
                    pe.wait_ge(lk_ready, 2 * (n * (SOLVE_STEPS - 1) + s) + half + 1)
                    for h in range(hs.start, hs.stop):
                        last = nc.tensor.matmul(solve_out[:, h, :], lt_diag[:, h, :], LU[:, h, :],
                                                start=True, stop=True)
                    last.then_inc(solve_mm, 1)

            def last_solve_step(g):
                for half, hs in enumerate(HALVES):
                    pe.wait_ge(u_next, 2 * (a0_index(g) + 1) * (SOLVE_STEPS - 1) - 1 + half)
                    blocks(lambda h, r: solve_out[r, h, S:2 * S], col(LT), lambda h, r: LU[r, h, S:2 * S],
                           hs).then_inc(solve_mm, 1)

            def attend(g):
                a = attn_index(g)
                pe.wait_ge(p_ready, a + 1)
                if a:
                    pe.wait_ge(o_ready, a)
                if a == 2 * TILES:
                    pe.wait_ge(fused, MT * TILES // CHUNK)
                if kind(g) == "a0":
                    pe.wait_ge(u_done, 2 * (a0_index(g) + 1))
                    rhs = lambda h, r: LU[r, h, S:2 * S]
                else:
                    pe.wait_ge(v_ready, a + 1)
                    rhs = lambda h, r: v_sb[r, g % 2, S * h:S * (h + 1)]
                if g + 1 in A0:
                    pe.wait_ge(beta_ready, a0_index(g + 1) + 1)
                blocks(col(ps[:, B_O, :]), col(pT), rhs).then_inc(pv_mm, 1)

            def a0_slot(g):
                k, v, y = k_project(g + 1), v_project(g + 1), out_project(g - 1)
                score_kk(g)
                issue(q_project(g + 1))
                if attends_late(g - 1):
                    attend(g - 1)
                issue(k, 8)
                solve_step(g, 0)
                o_transpose(g - 1)
                issue(k)
                solve_step(g, 1)
                issue(y, 2)
                issue(beta_project(g + 1))
                issue(y, 1)
                solve_step(g, 2)
                issue(y, 2)
                score_qk(g, 0)
                issue(y, 1)
                solve_step(g, 3)
                issue(y, 1)
                score_qk(g, 1)
                if transposed_here(g):
                    ln_transpose(g + 2)
                issue(y)
                last_solve_step(g)
                issue(v)

            def slot(g):
                if is_attn(g):
                    score(g)
                issue(q_project(g + 1))
                if attends_late(g - 1):
                    attend(g - 1)
                o_transpose(g - 1)
                issue(k_project(g + 1))
                issue(v_project(g + 1))
                issue(beta_project(g + 1))
                if transposed_here(g):
                    ln_transpose(g + 2)
                if is_attn(g) and not attends_late(g):
                    attend(g)
                issue(out_project(g - 1))
                sign_project(g)

            def gate_up(c, m):
                n = c * MT + m
                bank = GU_BANKS[n % 4]
                if n == 0:
                    pe.wait_ge(qk_ready, 2 * TILES)
                elif n == 2:
                    pe.wait_ge(shifted, 2 * TILES)
                elif n == 3:
                    pe.wait_ge(o_ready, 2 * TILES)
                if n >= 4:
                    pe.wait_ge(fused, n - 3)
                if m == 0:
                    pe.wait_ge(a_ready, 2 * TILES + CHUNK * (c + 1))
                for half, which in enumerate(("gate", "up")):
                    unit = UNIT[which + str(m // 4)]
                    pe.wait_ge(w_ready, unit + 1)
                    for k in range(KT):
                        for j, part in enumerate((a_hi, a_lo)):
                            col0 = 512 * k + P * (m % 4)
                            last = nc.tensor.matmul(
                                ps[:, bank, CHUNK * P * half:CHUNK * P * (half + 1)],
                                slot_mem(UNITS[unit][2][0])[:, col0:col0 + P], part[:, :, k, :],
                                start=(k == 0 and j == 0), stop=(k == KT - 1 and j == 1))
                last.then_inc(gu_mm, 1)

            pe.wait_ge(consts_loaded, 16)
            for g in RUN1[:-1]:
                a0_slot(g) if g in A0 else slot(g)
            gate_up(0, 0)
            attend(2 * TILES - 1)
            gate_up(0, 1)
            o_transpose(2 * TILES - 1)
            gate_up(0, 2)
            issue(out_project(2 * TILES - 1))
            for c in range(TILES // CHUNK):
                for m in range(3 if c == 0 else 0, MT):
                    gate_up(c, m)
                for i in range(CHUNK):
                    ln_transpose(2 * TILES + CHUNK * (c + 1) + i)
                for i in range(CHUNK):
                    n = CHUNK * c + i
                    if c == 0:
                        pe.wait_ge(u_done, 2 * TILES)
                    else:
                        pe.wait_ge(x_new, 2 * TILES + n - 1)
                    if i == 0:
                        pe.wait_ge(fuse_ready, MT * (c + 1))
                    for m in range(MT):
                        unit = UNIT["down" + str(m // 4)]
                        pe.wait_ge(w_ready, unit + 1)
                        for j in range(2):
                            last = nc.tensor.matmul(ps[:, B_S + i, :], fuse[:, j, m, P * i:P * (i + 1)],
                                                    weight(UNITS[unit][2][0], m % 4), start=(m == 0 and j == 0),
                                                    stop=(m == MT - 1 and j == 1))
                    last.then_inc(down_mm, 1)
            for g in RUN2:
                slot(g)
                if g == ALPHA_AT:
                    pe.wait_ge(abs_done, 1)
                    pe.wait_ge(pool_consts, 2)
                    pe.wait_ge(x_new, g)
                    for k in range(KT):
                        last = nc.tensor.matmul(ps[:, B_Y, :], ones[:], raw[:, UNIT["sign"] % 2, 512 * k:512 * (k + 1)],
                                                start=(k == 0), stop=(k == KT - 1))
                    last.then_inc(alpha_mm, 1)


def kernel(**inputs):
    import concourse.bacc as bacc
    from concourse.bass_utils import run_bass_kernel_spmd

    a = {k: np.asarray(v) for k, v in inputs.items()}
    nc = bacc.Bacc("TRN2", target_bir_lowering=False, num_devices=1)
    feed = {}

    def dram(name, array):
        feed[name] = np.ascontiguousarray(array)
        return nc.dram_tensor(name, feed[name].shape, mybir.dt.from_np(feed[name].dtype), kind="ExternalInput").ap()

    def units(ap, names, rows):
        blocks = {}
        for i, name in enumerate(names):
            part = ap[512 * i:512 * (i + 1), :] if rows else ap[:, 512 * i:512 * (i + 1)]
            blocks[name] = part.rearrange("(k p) n -> p k n", p=P)
        return blocks

    w = {}
    for s in "01":
        w |= units(dram(f"x{s}_wq", a[f"L{s}_xattn_Wq"].T), [f"x{s}q"], False)
        w[f"x{s}kv"] = dram(f"x{s}_wkv", a[f"L{s}_xattn_Wkv_expand"].T)
        w |= units(dram(f"x{s}_wo", a[f"L{s}_xattn_Wout"].T), [f"x{s}o"], False)
    for c in "qkvo":
        w |= units(dram(f"a0_w{c}", a[f"L0_attn_W{c}"]), [f"a0{c}"], False)
    w |= units(dram("gate_w", a["L0_ffn_gate_w"]), ["gate0", "gate1", "gate2"], False)
    w |= units(dram("up_w", a["L0_ffn_up_w"]), ["up0", "up1", "up2"], False)
    w |= units(dram("down_w", a["L0_ffn_down_w"]), ["down0", "down1", "down2"], True)
    w |= units(dram("a1_wqkv", a["L1_attn_qkv_w"].T), ["a1q", "a1k", "a1v"], False)
    w |= units(dram("a1_wo", a["L1_attn_out_w"].T), ["a1o"], False)
    w |= units(dram("f1_w", a["L1_ffn_weight"].T), ["sign"], False)
    vec = {
        "Wb": dram("Wb", a["L0_attn_Wb"]), "bb": dram("bb", a["L0_attn_bb"]),
        "slopes": dram("slopes", a["L1_attn_alibi_slopes"]), "down_scale": dram("down_scale", a["L0_ffn_down_scale"]),
        "gate_scale": dram("gate_scale", a["L0_ffn_gate_scale"].reshape(MT, P).T),
        "up_scale": dram("up_scale", a["L0_ffn_up_scale"].reshape(MT, P).T),
        "out_b": dram("out_b", a["L1_attn_out_b"]), "qkv_b": dram("qkv_b", a["L1_attn_qkv_b"]),
        "ffn_b": dram("ffn_b", a["L1_ffn_bias"]),
    }
    x = dram("x", a["x"].reshape(NB * S, H))
    ctxT = dram("ctxT", a["ctx_512"].transpose(2, 0, 1).reshape(CTX_L, NB * CTX_S))
    consts = dram("shape_constants", shape_constants())
    out = nc.dram_tensor("out", (NB * S, H), F32, kind="ExternalOutput").ap()
    build(nc, x, ctxT, consts, w, vec, out)
    r = run_bass_kernel_spmd(nc, [feed], core_ids=[0])
    return r.results[0]["out"].reshape(NB, S, H)
```
